# Optimizing a Trainium2 kernel written in Bass

```python
import numpy as np
import jax
import jax.numpy as jnp

def _softmax(x, axis=-1):
    return jax.nn.softmax(x, axis=axis)

def _gelu(x):
    return jax.nn.gelu(x, approximate=True)

def _silu(x):
    return jax.nn.silu(x)

def _sigmoid(x):
    return jax.nn.sigmoid(x)

def _layernorm(x, axis=-1, eps=1e-05):
    m = jnp.mean(x, axis=axis, keepdims=True)
    v = jnp.var(x, axis=axis, keepdims=True)
    return (x - m) / jnp.sqrt(v + eps)

def _scatter_add(tgt, idx, src, axis=0):
    return tgt.at[idx].add(src)

def _segment_sum(src, seg, n):
    return jax.ops.segment_sum(src, seg, n)
kernel_name = 'mk_adaln_attn_ffn_d1_seqx_r8_0d0b8c'

def setup_inputs(seed: int=0):
    np.random.seed(seed)
    _w = jnp.asarray

    def _rec_inputs():
        import jax
        import jax.numpy as jnp
        _rk = jax.random.key(seed)
        x = -7.109e-05 + 0.9999 * jax.random.normal(jax.random.fold_in(_rk, 1), (64, 32, 512), jnp.float32)
        _lenS = 32 - jax.random.randint(jax.random.fold_in(_rk, 7), (64,), 0, max(1, 32 // 4) + 1, jnp.int32)
        _lenS2 = 32 - jax.random.randint(jax.random.fold_in(_rk, 8), (64,), 0, max(1, 32 // 4) + 1, jnp.int32)
        itok_B_0_15 = jax.random.randint(jax.random.fold_in(_rk, 11), (64,), 0, 16, jnp.int32)
        condB_codebook = -0.0625 + 0.715345 * jax.random.normal(jax.random.fold_in(_rk, 12), (64,), jnp.float32)
        return (x, itok_B_0_15, condB_codebook)
    x, itok_B_0_15, condB_codebook = _rec_inputs()

    def _L0_cond_setup():
        import jax, jax.numpy as jnp
        import numpy as np
        B, C, T = (64, 32, 512)
        S, D = (16, 32)
        key = jax.random.key(seed)
        k1, k2, k3 = jax.random.split(key, 3)
        x = jax.random.normal(k1, (B, C, T), dtype=jnp.float32)
        condition = jax.random.randint(k2, (B,), 0, S, dtype=jnp.int64)
        bound = float(np.sqrt(6.0 / C))
        weights = jax.random.uniform(k3, (S, C, D), dtype=jnp.float32, minval=-bound, maxval=bound)
        return {'x': x, 'condition': condition, 'weights': weights}
    _L0_cond_all = _L0_cond_setup()
    _L0_cond_in = {k: v for k, v in _L0_cond_all.items() if k in ('weights',)}
    del _L0_cond_all

    def _L0_attn_setup():
        import jax, jax.numpy as jnp
        import numpy as np
        Q_DIM = 512
        N_HEADS = 32
        HEAD_DIM = 128
        INNER = N_HEADS * HEAD_DIM
        EPS = 1e-06

        def rms_norm(x, w):
            xf = x.astype(jnp.float32)
            var = jnp.mean(xf * xf, axis=-1, keepdims=True)
            return (w.astype(jnp.float32) * xf * jax.lax.rsqrt(var + EPS)).astype(x.dtype)
        key = jax.random.key(seed)
        ks = jax.random.split(key, 12)
        s = 1.0 / np.sqrt(Q_DIM)
        return {'hidden_states': jax.random.normal(ks[0], (2, 256, Q_DIM), dtype=jnp.float32), 'Wq': jax.random.normal(ks[1], (Q_DIM, INNER), dtype=jnp.float32) * s, 'bq': jnp.zeros((INNER,), dtype=jnp.float32), 'Wk': jax.random.normal(ks[2], (Q_DIM, INNER), dtype=jnp.float32) * s, 'bk': jnp.zeros((INNER,), dtype=jnp.float32), 'Wv': jax.random.normal(ks[3], (Q_DIM, INNER), dtype=jnp.float32) * s, 'bv': jnp.zeros((INNER,), dtype=jnp.float32), 'Wo': jax.random.normal(ks[4], (INNER, Q_DIM), dtype=jnp.float32) * s, 'bo': jnp.zeros((Q_DIM,), dtype=jnp.float32), 'gq': jnp.ones((INNER,), dtype=jnp.float32), 'gk': jnp.ones((INNER,), dtype=jnp.float32)}
    _L0_attn_all = _L0_attn_setup()
    _L0_attn_in = {k: v for k, v in _L0_attn_all.items() if k in ('Wq', 'bq', 'Wk', 'bk', 'Wv', 'bv', 'Wo', 'bo', 'gq', 'gk')}
    del _L0_attn_all

    def _L0_cond2_setup():
        import jax, jax.numpy as jnp
        import numpy as np
        GROUP = 128
        LORA_ALPHA = 32.0
        LORA_RANK = 64
        key = jax.random.key(seed)
        k1, k2, k3, k4 = jax.random.split(key, 4)
        O, I = (512, 512)
        x = jax.random.normal(k1, (4, 256, I), dtype=jnp.float32)
        weight = jax.random.normal(k2, (O, I), dtype=jnp.float32) * 0.02
        wg = weight.reshape(O, I // GROUP, GROUP)
        scale_log = jnp.log(jnp.clip(jnp.max(jnp.abs(wg), axis=2, keepdims=True), 1e-05))
        codebook = jnp.array([-1.0, -0.25, 0.0, 1.0], dtype=jnp.float32)
        lora_A = jax.random.normal(k3, (LORA_RANK, I), dtype=jnp.float32) * 0.02
        lora_B = jax.random.normal(k4, (O, LORA_RANK), dtype=jnp.float32) * 0.02
        return {'x': x, 'weight': weight, 'scale_log': scale_log, 'codebook': codebook, 'lora_A': lora_A, 'lora_B': lora_B}
    _L0_cond2_all = _L0_cond2_setup()
    _L0_cond2_in = {k: v for k, v in _L0_cond2_all.items() if k in ('weight', 'scale_log', 'lora_A', 'lora_B')}
    del _L0_cond2_all

    def _L0_ffn_setup():
        import jax, jax.numpy as jnp
        import numpy as np
        ALPHA = 32
        R = 16
        SCALING = ALPHA / R
        key = jax.random.key(seed)
        k1, k2, k3, k4 = jax.random.split(key, 4)
        B_, S, D = (4, 256, 512)
        H, r, O = (8, R, 512)
        x = jax.random.normal(k1, (B_, S, D), dtype=jnp.float32)
        A = jax.random.normal(k2, (H, r, D), dtype=jnp.float32) * 0.02
        Bm = jax.random.normal(k3, (H, O, r), dtype=jnp.float32) * 0.02
        Wr = jax.random.normal(k4, (H, D), dtype=jnp.float32) * 0.02
        br = jnp.zeros((H,), dtype=jnp.float32)
        return {'x': x, 'A': A, 'B': Bm, 'Wr': Wr, 'br': br}
    _L0_ffn_all = _L0_ffn_setup()
    _L0_ffn_in = {k: v for k, v in _L0_ffn_all.items() if k in ('A', 'B', 'Wr', 'br')}
    del _L0_ffn_all
    return {'x': x, 'itok_B_0_15': itok_B_0_15, 'condB_codebook': condB_codebook, 'L0_cond_weights': _L0_cond_in['weights'], 'L0_attn_Wq': _L0_attn_in['Wq'], 'L0_attn_bq': _L0_attn_in['bq'], 'L0_attn_Wk': _L0_attn_in['Wk'], 'L0_attn_bk': _L0_attn_in['bk'], 'L0_attn_Wv': _L0_attn_in['Wv'], 'L0_attn_bv': _L0_attn_in['bv'], 'L0_attn_Wo': _L0_attn_in['Wo'], 'L0_attn_bo': _L0_attn_in['bo'], 'L0_attn_gq': _L0_attn_in['gq'], 'L0_attn_gk': _L0_attn_in['gk'], 'L0_cond2_weight': _L0_cond2_in['weight'], 'L0_cond2_scale_log': _L0_cond2_in['scale_log'], 'L0_cond2_lora_A': _L0_cond2_in['lora_A'], 'L0_cond2_lora_B': _L0_cond2_in['lora_B'], 'L0_ffn_A': _L0_ffn_in['A'], 'L0_ffn_B': _L0_ffn_in['B'], 'L0_ffn_Wr': _L0_ffn_in['Wr'], 'L0_ffn_br': _L0_ffn_in['br']}

def reference(x, itok_B_0_15, condB_codebook, L0_cond_weights, L0_attn_Wq, L0_attn_bq, L0_attn_Wk, L0_attn_bk, L0_attn_Wv, L0_attn_bv, L0_attn_Wo, L0_attn_bo, L0_attn_gq, L0_attn_gk, L0_cond2_weight, L0_cond2_scale_log, L0_cond2_lora_A, L0_cond2_lora_B, L0_ffn_A, L0_ffn_B, L0_ffn_Wr, L0_ffn_br):
    import jax
    import jax.numpy as jnp

    def _L0_cond_ref(x, condition, weights):
        import jax, jax.numpy as jnp
        import numpy as np
        B, C, T = (64, 32, 512)
        S, D = (16, 32)
        W = weights[condition]
        return jnp.einsum('bct,bcd->bdt', x, W)

    def _L0_attn_ref(hidden_states, Wq, bq, Wk, bk, Wv, bv, Wo, bo, gq, gk):
        import jax, jax.numpy as jnp
        import numpy as np
        Q_DIM = 512
        N_HEADS = 32
        HEAD_DIM = 128
        INNER = N_HEADS * HEAD_DIM
        EPS = 1e-06

        def rms_norm(x, w):
            xf = x.astype(jnp.float32)
            var = jnp.mean(xf * xf, axis=-1, keepdims=True)
            return (w.astype(jnp.float32) * xf * jax.lax.rsqrt(var + EPS)).astype(x.dtype)
        B, S, _ = hidden_states.shape
        q = hidden_states @ Wq + bq
        k = hidden_states @ Wk + bk
        v = hidden_states @ Wv + bv
        q = rms_norm(q, gq)
        k = rms_norm(k, gk)
        q = q.reshape(B, S, N_HEADS, HEAD_DIM).transpose(0, 2, 1, 3)
        k = k.reshape(B, S, N_HEADS, HEAD_DIM).transpose(0, 2, 1, 3)
        v = v.reshape(B, S, N_HEADS, HEAD_DIM).transpose(0, 2, 1, 3)
        scale = 1.0 / np.sqrt(HEAD_DIM)
        attn = jnp.einsum('bhqd,bhkd->bhqk', q.astype(jnp.float32), k.astype(jnp.float32)) * scale
        attn = jax.nn.softmax(attn, axis=-1)
        out = jnp.einsum('bhqk,bhkd->bhqd', attn, v.astype(jnp.float32))
        out = out.transpose(0, 2, 1, 3).reshape(B, S, INNER).astype(hidden_states.dtype)
        return out @ Wo + bo

    def _L0_cond2_ref(x, weight, scale_log, codebook, lora_A, lora_B):
        import jax, jax.numpy as jnp
        import numpy as np
        GROUP = 128
        LORA_ALPHA = 32.0
        LORA_RANK = 64
        O, I = weight.shape
        lora_delta = lora_B @ lora_A * (LORA_ALPHA / LORA_RANK)
        cb = codebook / jnp.clip(jnp.max(jnp.abs(codebook)), 1e-08)
        scale = jnp.exp(scale_log)
        wg = (weight + lora_delta).reshape(O, I // GROUP, GROUP)
        normalized = wg / scale
        thresholds = (cb[:-1] + cb[1:]) * 0.5
        idx = jnp.searchsorted(thresholds, normalized, side='left')
        quantized = cb[idx]
        w = jax.lax.stop_gradient(quantized - normalized) + normalized
        w_q = (w * scale).reshape(O, I)
        w_eff = w_q + lora_delta
        return x @ w_eff.T

    def _L0_ffn_ref(x, A, B, Wr, br):
        import jax, jax.numpy as jnp
        import numpy as np
        ALPHA = 32
        R = 16
        SCALING = ALPHA / R
        H = A.shape[0]
        router_logits = jnp.einsum('bsd,hd->bsh', x, Wr) + br
        scores = H * jax.nn.softmax(router_logits, axis=-1)
        low = jnp.einsum('bsd,hrd->bshr', x, A)
        out = jnp.einsum('bshr,hor,bsh->bso', low, B, scores)
        return SCALING * out
    x = x + _L0_attn_ref(_L0_cond_ref(x, itok_B_0_15, L0_cond_weights), L0_attn_Wq, L0_attn_bq, L0_attn_Wk, L0_attn_bk, L0_attn_Wv, L0_attn_bv, L0_attn_Wo, L0_attn_bo, L0_attn_gq, L0_attn_gk)
    x = x + _L0_ffn_ref(_L0_cond2_ref(x, L0_cond2_weight, L0_cond2_scale_log, condB_codebook, L0_cond2_lora_A, L0_cond2_lora_B), L0_ffn_A, L0_ffn_B, L0_ffn_Wr, L0_ffn_br)
    return x

_drawn_inputs = setup_inputs


def setup_inputs(seed=0):
    import zlib

    import numpy as np

    out = dict(_drawn_inputs(seed))
    spreads = {'L0_attn_bq': (0.0, 0.1),
     'L0_attn_bk': (0.0, 0.8),
     'L0_attn_bv': (0.0, 0.1),
     'L0_attn_bo': (0.0, 0.1),
     'L0_attn_gq': (1.0, 0.2),
     'L0_attn_gk': (1.0, 0.2),
     'L0_ffn_br': (0.0, 0.521)}
    factors = {}
    for name, (base, spread) in spreads.items():
        noise = np.random.default_rng([zlib.crc32(name.encode()), seed]).standard_normal(out[name].shape)
        drawn = base * np.exp(spread * noise) if base else spread * noise
        out[name] = jnp.asarray(drawn.astype(out[name].dtype))
    for name, factor in factors.items():
        out[name] = (out[name] * factor).astype(out[name].dtype)
    return out
```

```python
from contextlib import ExitStack

import concourse.bass as bass
from concourse import mybir

F32 = mybir.dt.float32
F32R = mybir.dt.float32r
I32 = mybir.dt.int32
ALU = mybir.AluOpType
ACT = mybir.ActivationFunctionType
AX = mybir.AxisListType.X

P = 128
B, C, D = 64, 32, 512
KI = D // P
TOK = B * C
NT = TOK // P
NB = P // C
NCH = 4
TC = NT // NCH
CH = TC * P
H = 32
DH = 128
INNER = H * DH
S16 = 16
NP = H // 2
EPS = 1e-6
SCORE_SCALE = 1.0 / DH ** 0.5
G = 4
RANK = 64
LORA_SCALE = 32.0 / RANK
NCODE = 64
E_ = 8
R_ = 16
LR = E_ * R_ + E_
OUT_SCALE = E_ * (32.0 / R_)
BIG = 3.0e38
MAGIC = 12582912.0
LOG2E = 1.4426950408889634
LN2_HI, LN2_LO = 0.693359375, -2.12194440e-4
TAYLOR = [1 / 5040, 1 / 720, 1 / 120, 1 / 24, 1 / 6, 1 / 2, 1.0]

STEPS_A = H * NCH
PRO_A, LOOP_A = 12, 14
STEPS_B = NP * NCH
PRO_B, LOOP_B = 8, 6
UNITS_PRO = 14


def build(nc, x_nat, x_tr, cond_w, cond_idx, codebook, wqk, wvo, vecs, bo, w2, scale_log,
          lora_a, lora_bt, awr, bmat, br, out_t):
    spill = nc.dram_tensor("score_spill", (H, P, NT * C), F32, kind="Internal").ap()

    with ExitStack() as ctx:
        def sb(name, shape, dt=F32):
            return ctx.enter_context(nc.sbuf_tensor(name, shape, dt))

        def sem(name):
            return ctx.enter_context(nc.semaphore(name))

        xc_hi = sb("xc_hi", [P, KI, TOK], F32R)
        xc_lo = sb("xc_lo", [P, KI, TOK], F32R)
        xres = sb("xres", [P, KI * TOK])
        w_raw = sb("w_raw", [P, 2, 1024])
        vec = sb("vec", [P, H, 5])
        hv = sb("hv", [P, 2, 5])
        bvp = sb("bvp", [P, 2, 2])
        bo_sb = sb("bo_sb", [P, KI])
        ident = sb("ident", [P, P])
        ones = sb("ones", [P, P])
        awr_sb = sb("awr_sb", [P, KI, LR])
        lowmat = sb("lowmat", [P, KI, LR])
        b_sb = sb("b_sb", [P, D])
        br_sb = sb("br_sb", [P, E_])
        rqk = sb("rqk", [P, NT * C])
        mx = sb("mx", [P, 2 * NT])
        rsum = sb("rsum", [P, 2 * NT])
        rinv = sb("rinv", [P, 2 * NT])

        x_in = xres[:, :].rearrange("p (t f) -> p t f", t=NT)
        xr = xres[:, :].rearrange("p (i n) -> p i n", i=KI)

        with ExitStack() as mem_a:
            def sba(name, shape, dt=F32):
                return mem_a.enter_context(nc.sbuf_tensor(name, shape, dt))
            wa = sba("wa", [P, 2, 2, 1024], F32R)
            qk = sba("qk", [P, 2, 2, CH])
            sq = sba("sq", [P, 2, 2, CH])
            acc = sba("acc", [P, 2, TOK])
            stage = sba("stage", [P, 2, NT * C])
            qv = sba("qv", [P, KI * D])
            qf = sba("qf", [P, KI * D])
            qm = sba("qm", [P, 1024])
            mixw = sba("mixw", [P, NT, P])
            cw = acc[0:S16, :, :].rearrange("s a n -> s (a n)").rearrange("s (d j c) -> s d j c", d=C, j=NB)
            idx_i = sba("idx_i", [S16, B], I32)
            idx_f = sba("idx_f", [S16, B])
            row_i = sba("row_i", [S16, 1], I32)
            row_f = sba("row_f", [S16, 1])
            onehot = sba("onehot", [S16, B])
            cb = sba("cb", [P, NCODE])
            cbmax = sba("cbmax", [P, 2])
            thr = sba("thr", [P, NCODE + 1])
            thr_t = sba("thr_t", [P, NCODE])
            step = sba("step", [P, NCODE])
            sl = sba("sl", [P, KI * G])
            ek = sba("ek", [P, KI * G])
            er = sba("er", [P, KI * G])
            ep = sba("ep", [P, KI * G])
            e2i = sba("e2i", [P, KI * G], I32)
            gscale = sba("gscale", [P, KI * G])
            grec = sba("grec", [P, KI * G])
            la = sba("la", [RANK, D])
            lbt = sba("lbt", [RANK, D])
            kv = sba("kv", [P, NT * C])
            kn = sba("kn", [P, NT * C])
            kn2 = sba("kn2", [P, NT * C])
            qv1 = sba("qv1", [P, NT])
            qn = sba("qn", [P, NT])
            qn2 = sba("qn2", [P, NT])
        wb = sb("wb", [P, 2, 2, 2048], F32R)
        sc = sb("sc", [P, 2, 2 * NT * C])
        vb = sb("vb", [P, 2, TC, 2 * DH])
        pt = sb("pt", [P, 2, 2, TC, P])
        ot_hi = sb("ot_hi", [P, 2, 2, CH], F32R)
        ot_lo = sb("ot_lo", [P, 2, 2, CH], F32R)
        rl = vb[:, :, :, :].rearrange("p a t n -> p (a t n)")[:, 0:TC * LR].rearrange("p (t n) -> p t n", t=TC)
        sc_flat = sc[:, :, :].rearrange("p a n -> p (a n)")
        low_s = sc_flat[:, 0:CH].rearrange("p (t n) -> p t n", t=TC)
        low_t = sc_flat[:, CH:2 * CH]
        lmx = sc_flat[:, 2 * CH:2 * CH + 8]
        lsum = sc_flat[:, 2 * CH + 8:2 * CH + 16]
        linv = sc_flat[:, 2 * CH + 16:2 * CH + 24]
        lex = sc_flat[:, 2 * CH + 32:2 * CH + 64].rearrange("p (t e) -> p t e", t=TC)

        bank = [ctx.enter_context(nc.psum_tensor(f"bank{i}", [P, 512], F32)) for i in range(8)]

        ld_cond = sem("ld_cond")
        ld_x = [sem(f"ld_x{c}") for c in range(NCH)]
        ld_vec = sem("ld_vec")
        ld_quant = sem("ld_quant")
        ld_res = sem("ld_res")
        iota_done = sem("iota_done")
        const_done = sem("const_done")
        mix_zero = sem("mix_zero")
        mix_raw = sem("mix_raw")
        mix_done = sem("mix_done")
        onehot_done = sem("onehot_done")
        lora_done = sem("lora_done")
        lora_used = sem("lora_used")
        xc_raw = sem("xc_raw")
        xc_hi_done = sem("xc_hi_done")
        xc_lo_done = sem("xc_lo_done")
        vec_ready = sem("vec_ready")
        hv_ready = sem("hv_ready")
        bvp_ready = sem("bvp_ready")
        chain = sem("chain")
        wqk_loaded = [sem("wqk_loaded0"), sem("wqk_loaded1")]
        wqk_hi = sem("wqk_hi")
        wqk_lo = sem("wqk_lo")
        proj_done = sem("proj_done")
        qk_copied = sem("qk_copied")
        sq_ready = sem("sq_ready")
        acc_zero = sem("acc_zero")
        acc_done = sem("acc_done")
        scores_done = sem("scores_done")
        scores_kept = sem("scores_kept")
        spilled = [sem("spilled0"), sem("spilled1")]
        quant_mask = sem("quant_mask")
        quant_sum = sem("quant_sum")
        low_raw = sem("low_raw")
        low_ready = sem("low_ready")
        stat_done = sem("stat_done")
        var_ready = sem("var_ready")
        std_ready = sem("std_ready")
        rqk_ready = sem("rqk_ready")
        wvo_loaded = sem("wvo_loaded")
        wvo_hi = sem("wvo_hi")
        wvo_lo = sem("wvo_lo")
        res_ready = sem("res_ready")
        pt_zero = sem("pt_zero")
        sc_loaded = [sem("sc_loaded0"), sem("sc_loaded1")]
        sm_scaled = sem("sm_scaled")
        sm_max = sem("sm_max")
        sm_shift = sem("sm_shift")
        sm_exp = sem("sm_exp")
        sm_sum = sem("sm_sum")
        sm_rinv = sem("sm_rinv")
        p_ready = sem("p_ready")
        pt_ready = sem("pt_ready")
        v_done = sem("v_done")
        v_kept = sem("v_kept")
        pv_done = sem("pv_done")
        o_hi = sem("o_hi")
        o_lo = sem("o_lo")
        wo_done = sem("wo_done")
        wo_added = sem("wo_added")
        rl_done = sem("rl_done")
        logit_shift = sem("logit_shift")
        logit_exp = sem("logit_exp")
        low_scaled = sem("low_scaled")
        lowt_raw = sem("lowt_raw")
        lowt_done = sem("lowt_done")
        fin_raw = sem("fin_raw")
        fin_done = sem("fin_done")
        stored = sem("stored")

        def scores_view(ap):
            return ap.rearrange("p (h t k) -> p h t k", h=2, t=NT)

        block = ctx.enter_context(nc.Block())

        @block.sync
        def _(sp):
            for j in range(NB):
                sp.dma_start(cw[:, :, j, :], cond_w).then_inc(ld_cond, 16)
            sp.dma_start(idx_i[:, :], cond_idx).then_inc(ld_cond, 16)
            for c in range(NCH):
                sp.dma_start(x_in[:, c * TC:(c + 1) * TC, :], x_nat[:, c * TC:(c + 1) * TC, :]).then_inc(ld_x[c], 16)
                if c == 0:
                    for h in range(2):
                        sp.dma_start(w_raw[:, h, :], wqk[h]).then_inc(wqk_loaded[h], 16)
                    sp.dma_start(vec[:, :, :], vecs).then_inc(ld_vec, 16)
            for dst, src in ((cb[:, :], codebook), (sl[:, :], scale_log), (la[:, :], lora_a),
                             (lbt[:, :], lora_bt), (qv[:, :], w2), (awr_sb[:, :, :], awr),
                             (b_sb[:, :], bmat), (br_sb[:, :], br), (bo_sb[:, :], bo)):
                sp.dma_start(dst, src).then_inc(ld_quant, 16)
            sp.wait_ge(xc_raw, NT)
            sp.dma_start(xr, x_tr).then_inc(ld_res, 16)

            def load_head(h, hr, split_count):
                sp.wait_ge(wqk_lo, split_count)
                sp.dma_start(w_raw[:, hr % 2, :], wqk[h]).then_inc(wqk_loaded[hr % 2], 16)

            def spill_head(h, hr, kept_count):
                sp.wait_ge(scores_kept, kept_count)
                sp.dma_start(spill[h], stage[:, hr % 2, :]).then_inc(spilled[hr % 2], 16)

            for h in range(3):
                load_head(h + 2, h, h + 1)
                spill_head(h, h, 4 * h + 4)
            with sp.Fori(0, LOOP_A - 1) as i:
                for r in range(2):
                    load = sp.snap(2 * i + (5 + r))
                    store = sp.snap(2 * i + (3 + r))
                    split = sp.snap(2 * i + (4 + r))
                    kept = sp.snap(8 * i + (16 + 4 * r))
                    sp.wait_ge(wqk_lo, split)
                    sp.dma_start(w_raw[:, (1 + r) % 2, :], wqk[bass.ds(load, 1)].rearrange("a p n -> (a p) n"))\
                      .then_inc(wqk_loaded[(1 + r) % 2], 16)
                    sp.wait_ge(scores_kept, kept)
                    sp.dma_start(spill[bass.ds(store, 1)].rearrange("a p n -> (a p) n"), stage[:, (1 + r) % 2, :])\
                      .then_inc(spilled[(1 + r) % 2], 16)
            load_head(H - 1, H - 1, H - 2)
            spill_head(H - 3, H - 3, 4 * (H - 2))
            w_all = w_raw[:, :, :].rearrange("p a n -> p (a n)")
            sp.wait_ge(wqk_lo, H)
            sp.dma_start(w_all, wvo[0]).then_inc(wvo_loaded, 16)
            spill_head(H - 2, H - 2, 4 * (H - 1))
            spill_head(H - 1, H - 1, 4 * H)

            sp.wait_ge(spilled[0], 16 * NP)
            sp.wait_ge(spilled[1], 16 * NP)

            def load_scores(q):
                if q >= 2:
                    sp.wait_ge(pt_ready, 4 * q - 4)
                sp.dma_start(sc[:, q % 2, :].rearrange("p (a n) -> p a n", a=2),
                             spill[2 * q:2 * q + 2].rearrange("a p n -> p a n")).then_inc(sc_loaded[q % 2], 16)

            def load_wvo(p):
                sp.wait_ge(wvo_lo, 2 * p)
                sp.dma_start(w_all, wvo[p]).then_inc(wvo_loaded, 16)

            sp.wait_ge(rqk_ready, 1)
            sp.wait_ge(low_ready, 1)
            load_scores(0)
            load_wvo(1)
            load_scores(1)
            load_wvo(2)
            load_scores(2)
            load_wvo(3)
            load_scores(3)
            with sp.Fori(0, LOOP_B) as i:
                for r in range(2):
                    pair = sp.snap(2 * i + (4 + r))
                    half = sp.snap(4 * i + (8 + 2 * r))
                    parts = sp.snap(4 * i + (8 + 2 * r))
                    used = sp.snap(8 * i + (12 + 4 * r))
                    sp.wait_ge(wvo_lo, parts)
                    sp.dma_start(w_all, wvo[bass.ds(pair, 1)].rearrange("a p n -> (a p) n")).then_inc(wvo_loaded, 16)
                    sp.wait_ge(pt_ready, used)
                    sp.dma_start(sc[:, r, :].rearrange("p (a n) -> p a n", a=2),
                                 spill[bass.ds(half, 2)].rearrange("a p n -> p a n")).then_inc(sc_loaded[r], 16)

            for c in range(NCH):
                for i in range(KI):
                    n = c * KI + i
                    sp.wait_ge(fin_done, n + 1)
                    sp.dma_start(out_t[:, i, c * CH:(c + 1) * CH], xr[:, i, c * CH:(c + 1) * CH]).then_inc(stored, 16)
            sp.wait_ge(stored, 16 * NCH * KI)

        @block.tensor
        def _(pe):
            pe.wait_ge(ld_cond, 16 * (NB + 1))
            pe.wait_ge(onehot_done, 1)
            for d in range(C):
                ins = pe.matmul(bank[d // 8][:, (d % 8) * B:(d % 8 + 1) * B],
                                cw[:, d, :, :].rearrange("s j c -> s (j c)"), onehot[:, :], start=True, stop=True)
            ins.then_inc(mix_raw, 1)
            pe.wait_ge(mix_done, NB * 4)
            for c in range(NCH):
                pe.wait_ge(ld_x[c], 16)
                for i in range(KI):
                    n = c * KI + i
                    if n >= 4:
                        pe.wait_ge(xc_lo_done, n - 3)
                    for t in range(TC):
                        ins = pe.matmul(bank[n % 4][:, t * P:(t + 1) * P], x_in[:, c * TC + t, i * P:(i + 1) * P],
                                        mixw[:, c * TC + t, :], start=True, stop=True)
                    ins.then_inc(xc_raw, 1)

            def lora(ob):
                pe.matmul(bank[6 + ob % 2][:, :], lbt[:, ob * P:(ob + 1) * P], la[:, :],
                          start=True, stop=True).then_inc(lora_done, 1)

            pe.wait_ge(ld_quant, 16 * 9)
            for ob in range(KI):
                if ob >= 2:
                    pe.wait_ge(lora_used, ob - 1)
                lora(ob)

            def project(s, r, kind):
                u = 2 * r + kind
                hs, n = (r // NCH) % 2, r % NCH
                dst = bank[u % 4][:, :]
                k = 0
                for i in range(KI):
                    col = kind * 512 + i * P
                    for wpart, xpart in ((0, xc_hi), (0, xc_lo), (1, xc_hi)):
                        ins = pe.matmul(dst, wa[:, hs, wpart, col:col + P], xpart[:, i, n * CH:(n + 1) * CH],
                                        start=(k == 0), stop=(k == 11))
                        k += 1
                ins.then_inc(proj_done, 1)

            def scores(s, r):
                for t in range(TC):
                    ins = pe.matmul(bank[4 + r % 2][:, t * P:(t + 1) * P], qk[:, r % 2, 0, t * P:(t + 1) * P],
                                    qk[:, r % 2, 1, t * P:(t + 1) * P], start=True, stop=True)
                ins.then_inc(scores_done, 1)

            def step_a(s, r, first=0):
                if r % NCH == 0:
                    if isinstance(s, int):
                        pe.wait_ge(wqk_lo, s // NCH + 1)
                    else:
                        pe.wait_ge(wqk_lo, first)
                if not isinstance(s, int) or s >= 2:
                    pe.wait_ge(sq_ready, 2 * s - 3)
                elif s == 0:
                    pe.wait_ge(xc_lo_done, NCH * KI)
                    pe.wait_ge(xc_hi_done, NCH * KI)
                project(s, r, 0)
                if not isinstance(s, int) or s >= 1:
                    scores_when(s - 1, r + 7)
                if not isinstance(s, int) or s >= 2:
                    pe.wait_ge(sq_ready, 2 * s - 2)
                project(s, r, 1)

            def scores_when(s, r):
                pe.wait_ge(qk_copied, 2 * s + 2)
                if not isinstance(s, int) or s >= 2:
                    pe.wait_ge(scores_kept, s - 1)
                scores(s, r)

            for s in range(PRO_A):
                step_a(s, s % 8)
            with pe.Fori(0, LOOP_A) as i:
                for r in range(8):
                    step_a(8 * i + (PRO_A + r), (PRO_A + r) % 8, 2 * i + (4 + r // NCH))
            for s in range(STEPS_A - NCH, STEPS_A):
                step_a(s, s % 8)
                if s in (STEPS_A - 4, STEPS_A - 1):
                    for ob in ((0, 1) if s == STEPS_A - 4 else (2, 3)):
                        pe.wait_ge(lora_used, ob + 3)
                        lora(ob)
            scores_when(STEPS_A - 1, (STEPS_A - 1) % 8)
            pe.wait_ge(acc_done, 2 * STEPS_A)
            pe.wait_ge(scores_kept, STEPS_A - 1)
            for t in range(NT):
                pe.matmul(bank[4][:, t:t + 1], acc[:, 0, t * P:(t + 1) * P], ones[:, 0:1], start=True, stop=True)
            pe.wait_ge(sq_ready, 2 * STEPS_A)
            for c in range(NCH):
                ins = pe.matmul(bank[c][:, :], ones[:, :], acc[:, 1, c * CH:(c + 1) * CH], start=True, stop=True)
            ins.then_inc(stat_done, 1)
            pe.wait_ge(lora_used, 2 * KI)
            for i in range(KI):
                for ob in range(KI):
                    ins = pe.matmul(bank[6 + i // 2][:, (i % 2) * LR:(i % 2 + 1) * LR],
                                    qf[:, ob * D + i * P:ob * D + (i + 1) * P], awr_sb[:, ob, :],
                                    start=(ob == 0), stop=(ob == KI - 1))
            ins.then_inc(low_raw, 1)

            def v_half(g, r, half):
                slot, n = (r // NCH) % 2, r % NCH
                if not isinstance(g, int) or g >= 1:
                    pe.wait_ge(v_kept, 2 * g + (half - 1))
                for t in range(2):
                    tile = n * TC + half * 2 + t
                    k = 0
                    for i in range(KI):
                        for xpart, wpart in ((xc_hi, 0), (xc_hi, 1), (xc_lo, 0)):
                            ins = pe.matmul(bank[half][:, t * 256:(t + 1) * 256], xpart[:, i, tile * P:(tile + 1) * P],
                                            wb[:, slot, wpart, i * 256:(i + 1) * 256], start=(k == 0), stop=(k == 11))
                            k += 1
                ins.then_inc(v_done, 1)

            def pv(g, r, h):
                if h == 0:
                    pe.wait_ge(v_kept, 2 * g + 2)
                    pe.wait_ge(pt_ready, g + 1)
                if not isinstance(g, int) or g >= 1:
                    pe.wait_ge(o_lo, 2 * g + (h - 1))
                for t in range(TC):
                    ins = pe.matmul(bank[2 + h][:, t * P:(t + 1) * P], vb[:, r % 2, t, h * DH:(h + 1) * DH],
                                    pt[:, r % 2, h, t, :], start=True, stop=True)
                ins.then_inc(pv_done, 1)

            def project_out(g, r):
                slot = (r // NCH) % 2
                pe.wait_ge(o_lo, 2 * g + 2)
                for i in range(KI):
                    if not isinstance(g, int) or g >= 1:
                        pe.wait_ge(wo_added, 4 * g + (i - 3))
                    k = 0
                    for h in range(2):
                        col = 1024 + h * D + i * P
                        for wpart, opart in ((0, ot_hi), (0, ot_lo), (1, ot_hi)):
                            ins = pe.matmul(bank[4 + i][:, :], wb[:, slot, wpart, col:col + P],
                                            opart[:, r % 2, h, :], start=(k == 0), stop=(k == 5))
                            k += 1
                    ins.then_inc(wo_done, 1)

            def step_b(g, r, wv_parts=None, wo_parts=None):
                static = isinstance(g, int)
                if r % NCH == 0:
                    pe.wait_ge(wvo_lo, 2 * (g // NCH) + 1 if static else wv_parts)
                v_half(g, r, 0)
                if not static or g >= 1:
                    pv(g - 1, r + 7, 0)
                v_half(g, r, 1)
                if not static or g >= 1:
                    pv(g - 1, r + 7, 1)
                if r % NCH == 2 and (not static or g >= 2):
                    pe.wait_ge(wvo_lo, 2 * ((g - 2) // NCH) + 2 if static else wo_parts)
                if not static or g >= 2:
                    project_out(g - 2, r + 6)

            pe.wait_ge(var_ready, 2)
            for g in range(PRO_B):
                if g == 2:
                    pe.wait_ge(low_ready, 1)
                step_b(g, g)
            with pe.Fori(0, LOOP_B) as i:
                for r in range(8):
                    step_b(8 * i + (PRO_B + r), r, 4 * i + (5 + 2 * (r // NCH)), 4 * i + (6 + 2 * (r // NCH)))
            for g in range(PRO_B + 8 * LOOP_B, STEPS_B):
                step_b(g, g % 8)
            last = STEPS_B - 1
            pv(last, last % 8, 0)
            pv(last, last % 8, 1)
            project_out(last - 1, (last - 1) % 8)
            project_out(last, last % 8)

            for c in range(NCH):
                if c == 0:
                    pe.wait_ge(wo_added, 4 * STEPS_B)
                for t in range(TC):
                    for i in range(KI):
                        n = c * TC + t
                        ins = pe.matmul(bank[2 * c + t // 2][:, (t % 2) * LR:(t % 2 + 1) * LR],
                                        xr[:, i, n * P:(n + 1) * P], lowmat[:, i, :], start=(i == 0), stop=(i == KI - 1))
                ins.then_inc(rl_done, 1)
            for c in range(NCH):
                pe.wait_ge(low_scaled, c + 1)
                for t in range(TC):
                    ins = pe.transpose(bank[2 * c][:, t * P:(t + 1) * P], low_s[:, t, :], ident[:, :])
                ins.then_inc(lowt_raw, 1)
                pe.wait_ge(lowt_done, c + 1)
                for i in range(KI):
                    if i >= 2:
                        pe.wait_ge(fin_done, c * KI + i - 1)
                    pe.matmul(bank[2 * c + 1 - i % 2][:, :], b_sb[:, i * P:(i + 1) * P], low_t,
                              start=True, stop=True).then_inc(fin_raw, 1)

        @block.scalar
        def _(act):
            def wqk_part(h, hr, load_count, free_count):
                act.wait_ge(wqk_loaded[hr % 2], load_count)
                if free_count is not None:
                    act.wait_ge(proj_done, free_count)
                act.activation(wa[:, hr % 2, 0, :], w_raw[:, hr % 2, :], ACT.Copy).then_inc(wqk_hi, 1)

            for n in range(NCH * KI):
                c, i = n // KI, n % KI
                act.wait_ge(xc_raw, n + 1)
                act.activation(xc_hi[:, i, c * CH:(c + 1) * CH], bank[n % 4][:, :], ACT.Copy).then_inc(xc_hi_done, 1)
                if n == 0:
                    wqk_part(0, 0, 16, None)
                if n == 4:
                    wqk_part(1, 1, 16, None)

            def step_a(s, r, h, load_count):
                static = isinstance(s, int)
                hs = (r // NCH) % 2
                if r % NCH == 0:
                    act.activation(hv[:, hs:hs + 1, :], vec[:, bass.ds(h, 1), :], ACT.Copy).then_inc(hv_ready, 1)
                    act.wait_ge(hv_ready, h + 1)
                for kind in range(2):
                    u = 2 * r + kind
                    act.wait_ge(proj_done, 2 * s + (1 + kind))
                    if kind == 0 and (not static or s >= 2):
                        act.wait_ge(scores_done, s - 1)
                    scale = hv[:, hs, 3:4] if kind == 0 else 1.0
                    bias = hv[:, hs, 4:5] if kind == 0 else hv[:, hs, 1:2]
                    act.activation(qk[:, r % 2, kind, :], bank[u % 4][:, :], ACT.Identity, bias=bias, scale=scale)\
                       .then_inc(qk_copied, 1)
                    if not static or s >= 2:
                        act.wait_ge(acc_done, 2 * s + (kind - 3))
                    act.activation(sq[:, r % 2, kind, :], bank[u % 4][:, :], ACT.Square,
                                   bias=hv[:, hs, kind:kind + 1], scale=1.0).then_inc(sq_ready, 1)
                if r % NCH == 1 and not (static and s // NCH + 1 >= H):
                    if static:
                        hh = s // NCH + 1
                        if hh >= 2:
                            wqk_part(hh, hh, 16 * (hh // 2 + 1), 8 * (hh - 1))
                    else:
                        wqk_part(None, r // NCH + 1, load_count, 2 * s - 2)

            act.wait_ge(vec_ready, 2)
            for s in range(PRO_A):
                step_a(s, s % 8, s // NCH, None)
            with act.Fori(0, LOOP_A) as i:
                for r in range(8):
                    if r % NCH == 0:
                        hreg = act.snap(2 * i + (3 + r // NCH))
                    step_a(8 * i + (PRO_A + r), (PRO_A + r) % 8, hreg, 16 * i + 48)
            for s in range(STEPS_A - NCH, STEPS_A):
                step_a(s, s % 8, s // NCH, None)

            def wvo_part(p, r, part, load_count, free_sem, free_count):
                act.wait_ge(wvo_loaded, load_count)
                if free_sem is not None:
                    act.wait_ge(free_sem, free_count)
                act.activation(wb[:, r % 2, 0, part * 1024:(part + 1) * 1024], w_all[:, part * 1024:(part + 1) * 1024],
                               ACT.Copy).then_inc(wvo_hi, 1)

            w_all = w_raw[:, :, :].rearrange("p a n -> p (a n)")
            act.wait_ge(scores_done, STEPS_A)
            act.wait_ge(acc_done, 2 * STEPS_A)
            wvo_part(0, 0, 0, 16, None, None)
            wvo_part(0, 0, 1, 16, None, None)
            act.wait_ge(var_ready, 2)
            act.activation(qn[:, :], qv1[:, :], ACT.Sqrt).then_inc(std_ready, 1)
            act.activation(kn[:, :], kv[:, :], ACT.Sqrt).then_inc(std_ready, 1)
            act.wait_ge(low_raw, 1)
            act.activation(lowmat[:, 0:2, :], bank[6][:, 0:2 * LR].rearrange("p (i n) -> p i n", i=2), ACT.Copy)
            act.activation(lowmat[:, 2:4, :], bank[7][:, 0:2 * LR].rearrange("p (i n) -> p i n", i=2), ACT.Copy)\
               .then_inc(low_ready, 1)

            def exps(q, qr):
                act.wait_ge(sm_shift, q + 1)
                act.activation(sc[:, qr % 2, :], sc[:, qr % 2, :], ACT.Exp).then_inc(sm_exp, 1)

            exps(0, 0)

            def copy_v(g, r, half):
                act.wait_ge(v_done, 2 * g + (half + 1))
                if half == 0 and (not isinstance(g, int) or g >= 2):
                    act.wait_ge(pv_done, 2 * g - 2)
                act.activation(vb[:, r % 2, 2 * half:2 * half + 2, :],
                               bank[half][:, :].rearrange("p (t n) -> p t n", t=2), ACT.Copy).then_inc(v_kept, 1)

            def pair_bias(p, pr, head):
                act.activation(bvp[:, pr % 2, :], vec[:, bass.ds(head, 2), 2], ACT.Copy).then_inc(bvp_ready, 1)
                act.wait_ge(bvp_ready, p + 1)

            def out_hi(g, r, h):
                act.wait_ge(pv_done, 2 * g + (h + 1))
                if h == 0 and (not isinstance(g, int) or g >= 2):
                    act.wait_ge(wo_done, 4 * g - 4)
                act.activation(ot_hi[:, r % 2, h, :], bank[2 + h][:, :], ACT.Identity,
                               bias=bvp[:, (r // NCH) % 2, h:h + 1], scale=1.0).then_inc(o_hi, 1)

            def step_b(g, r, loaded, pair, head=None, last=False):
                static = isinstance(g, int)
                copy_v(g, r, 0)
                if not static or g >= 1:
                    out_hi(g - 1, r + 7, 0)
                copy_v(g, r, 1)
                if not static or g >= 1:
                    out_hi(g - 1, r + 7, 1)
                if r % NCH == 0:
                    pair_bias(pair - 1, r // NCH, head)
                if not last:
                    if r % NCH == 1:
                        wvo_part(None, r // NCH + 1, 0, loaded, v_done, 2 * g - 2) if (not static or g > 1) else \
                            wvo_part(None, r // NCH + 1, 0, loaded, None, None)
                        exps(pair, r // NCH + 1)
                    if r % NCH == 2:
                        wvo_part(None, r // NCH + 1, 1, loaded, wo_done, 4 * g - 8) if (not static or g > 2) else \
                            wvo_part(None, r // NCH + 1, 1, loaded, None, None)

            for g in range(PRO_B):
                p = g // NCH
                step_b(g, g, 16 * (p + 2), p + 1, 2 * p)
            with act.Fori(0, LOOP_B) as i:
                for r in range(8):
                    if r % NCH == 0:
                        head = act.snap(4 * i + (4 + 2 * (r // NCH)))
                    step_b(8 * i + (PRO_B + r), r, 32 * i + (64 + 16 * (r // NCH)), 2 * i + (3 + r // NCH), head)
            for g in range(PRO_B + 8 * LOOP_B, STEPS_B):
                p = g // NCH
                step_b(g, g % 8, 16 * (p + 2), p + 1, 2 * p, last=p == NP - 1)
            out_hi(STEPS_B - 1, (STEPS_B - 1) % 8, 0)
            out_hi(STEPS_B - 1, (STEPS_B - 1) % 8, 1)

            for c in range(NCH):
                act.wait_ge(logit_shift, c + 1)
                act.activation(lex, lex, ACT.Exp).then_inc(logit_exp, 1)
                act.wait_ge(lowt_raw, c + 1)
                act.activation(low_t, bank[2 * c][:, :], ACT.Copy).then_inc(lowt_done, 1)

        @block.gpsimd
        def _(pool):
            pool.iota(row_i[:, :], pattern=[[0, 1]], base=0, channel_multiplier=1).then_inc(iota_done, 1)
            pool.memset(mixw[:, :, :], 0.0).then_inc(mix_zero, 1)
            pool.memset(ones[:, :], 1.0).then_inc(const_done, 1)
            pool.memset(ident[:, :], 0.0).then_inc(const_done, 1)
            pool.wait_ge(const_done, 2)
            pool.affine_select(out=ident[:, :], in_=ident[:, :], compare_op=ALU.not_equal, fill=1.0,
                               base=0, pattern=[[-1, P]], channel_multiplier=1).then_inc(const_done, 1)
            pool.wait_ge(mix_raw, 1)
            pool.memset(acc[:, :, :], 0.0).then_inc(acc_zero, 1)
            pool.wait_ge(acc_zero, 1)

            def wqk_part(hr, count):
                pool.wait_ge(wqk_hi, count)
                pool.tensor_tensor(wa[:, hr % 2, 1, :], w_raw[:, hr % 2, :], wa[:, hr % 2, 0, :].bitcast(F32),
                                   ALU.subtract).then_inc(wqk_lo, 1)

            wqk_part(0, 1)
            wqk_part(1, 2)

            def step_a(s, r, part_count):
                static = isinstance(s, int)
                n = r % NCH
                for kind in range(2):
                    pool.wait_ge(sq_ready, 2 * s + (1 + kind))
                    if not static or s >= 4:
                        pool.wait_ge(acc_done, 2 * s + (kind - 7))
                    a = acc[:, kind, n * CH:(n + 1) * CH]
                    pool.tensor_tensor(a, a, sq[:, r % 2, kind, :], ALU.add).then_inc(acc_done, 1)
                if n == 1:
                    if static:
                        if 2 <= s // NCH + 1 < H:
                            wqk_part(s // NCH + 1, s // NCH + 2)
                    else:
                        wqk_part(r // NCH + 1, part_count)

            for s in range(PRO_A):
                step_a(s, s % 8, None)
            with pool.Fori(0, LOOP_A) as i:
                for r in range(8):
                    step_a(8 * i + (PRO_A + r), (PRO_A + r) % 8, 2 * i + (5 + r // NCH))
            for s in range(STEPS_A - NCH, STEPS_A):
                step_a(s, s % 8, None)

            w_all = w_raw[:, :, :].rearrange("p a n -> p (a n)")
            def wvo_part(r, part, count):
                pool.wait_ge(wvo_hi, count)
                cols = slice(part * 1024, (part + 1) * 1024)
                pool.tensor_tensor(wb[:, r % 2, 1, cols], w_all[:, cols], wb[:, r % 2, 0, cols].bitcast(F32),
                                   ALU.subtract).then_inc(wvo_lo, 1)

            wvo_part(0, 0, 1)
            wvo_part(0, 1, 2)
            pool.wait_ge(spilled[0], 16 * NP)
            pool.wait_ge(spilled[1], 16 * NP)
            pool.wait_ge(low_ready, 1)
            pool.memset(pt[:, :, :, :, :], 0.0).then_inc(pt_zero, 1)

            def scale_scores(q, qr, load_count):
                pool.wait_ge(sc_loaded[qr % 2], load_count)
                v = sc[:, qr % 2, :].rearrange("p (h n) -> p h n", h=2)
                pool.tensor_tensor(v, v, rqk[:, :].unsqueeze(1).broadcast_to([P, 2, NT * C]), ALU.mult)\
                    .then_inc(sm_scaled, 1)

            def normalise(q, qr):
                pool.wait_ge(sm_rinv, q + 1)
                v = sc[:, qr % 2, :].rearrange("p (m k) -> p m k", k=C)
                pool.tensor_tensor(v, v, rinv[:, :].unsqueeze(2).broadcast_to([P, 2 * NT, C]), ALU.mult)\
                    .then_inc(p_ready, 1)

            scale_scores(0, 0, 16)
            normalise(0, 0)

            def pair_b(q, qr, load_count, part_count):
                scale_scores(q, qr, load_count)
                wvo_part(qr, 0, part_count)
                wvo_part(qr, 1, part_count + 1)
                normalise(q, qr)

            for q in (1, 2):
                pair_b(q, q, 16 * (q // 2 + 1), 2 * q + 1)
            with pool.Fori(0, LOOP_B) as i:
                for r in range(2):
                    pair_b(2 * i + (3 + r), 3 + r, 16 * i + (32 + 16 * r), 4 * i + (7 + 2 * r))
            pair_b(NP - 1, NP - 1, 16 * (NP // 2), 2 * NP - 1)

        @block.vector
        def _(dve):
            chained = [0]

            def link(ins):
                chained[0] += 1
                ins.then_inc(chain, 1)
                dve.wait_ge(chain, chained[0])

            dve.wait_ge(ld_cond, 16 * (NB + 1))
            dve.wait_ge(iota_done, 1)
            link(dve.tensor_copy(idx_f[:, :], idx_i[:, :]))
            link(dve.tensor_copy(row_f[:, :], row_i[:, :]))
            dve.tensor_scalar(onehot[:, :], idx_f[:, :], row_f[:, 0:1], None, ALU.is_equal).then_inc(onehot_done, 1)

            dve.wait_ge(mix_raw, 1)
            dve.wait_ge(mix_zero, 1)
            for j in range(NB):
                rows = slice(j * C, (j + 1) * C)
                for b4 in range(4):
                    src = bank[b4][rows, :].rearrange("p (d t j) -> p j t d", t=NT, j=NB)[:, j]
                    dve.tensor_copy(mixw[rows, :, j * C + b4 * 8:j * C + b4 * 8 + 8], src).then_inc(mix_done, 1)

            for n in range(NCH * KI):
                c, i = n // KI, n % KI
                dve.wait_ge(xc_hi_done, n + 1)
                dst = (i, slice(c * CH, (c + 1) * CH))
                dve.tensor_tensor(xc_lo[:, dst[0], dst[1]], bank[n % 4][:, :], xc_hi[:, dst[0], dst[1]].bitcast(F32),
                                  ALU.subtract).then_inc(xc_lo_done, 1)
                if n == 0:
                    dve.wait_ge(ld_vec, 16)
                    dve.tensor_tensor(vec[:, :, 3], vec[:, :, 3], vec[:, :, 4], ALU.mult).then_inc(vec_ready, 1)
                    dve.wait_ge(vec_ready, 1)
                    dve.tensor_tensor(vec[:, :, 4], vec[:, :, 0], vec[:, :, 3], ALU.mult).then_inc(vec_ready, 1)

            dve.wait_ge(ld_quant, 16 * 9)
            link(dve.tensor_reduce(cbmax[:, 0:1], cb[:, :], AX, ALU.max, apply_absolute_value=True))
            link(dve.tensor_scalar(cbmax[:, 0:1], cbmax[:, 0:1], 1e-8, None, ALU.max))
            link(dve.reciprocal(cbmax[:, 1:2], cbmax[:, 0:1]))
            link(dve.tensor_scalar(cb[:, :], cb[:, :], cbmax[:, 1:2], None, ALU.mult))
            link(dve.tensor_tensor(step[:, 0:NCODE - 1], cb[:, 1:NCODE], cb[:, 0:NCODE - 1], ALU.subtract))
            link(dve.tensor_tensor(thr_t[:, 0:NCODE - 1], cb[:, 1:NCODE], cb[:, 0:NCODE - 1], ALU.add))
            link(dve.memset(thr[:, 0:1], -BIG))
            link(dve.memset(thr[:, NCODE:NCODE + 1], BIG))
            link(dve.tensor_scalar(thr[:, 1:NCODE], thr_t[:, 0:NCODE - 1], 0.5, None, ALU.mult))
            s = NCODE // 2
            while s >= 1:
                mid, low, high = thr[:, s:NCODE:2 * s], thr[:, 0:NCODE:2 * s], thr[:, 2 * s:NCODE + 1:2 * s]
                link(dve.tensor_tensor(mid, mid, low, ALU.max))
                link(dve.tensor_tensor(mid, mid, high, ALU.min))
                s //= 2
            link(dve.tensor_scalar(sl[:, :], sl[:, :], 88.0, -87.0, ALU.min, ALU.max))
            link(dve.tensor_scalar(ek[:, :], sl[:, :], LOG2E, MAGIC, ALU.mult, ALU.add))
            link(dve.tensor_scalar(ek[:, :], ek[:, :], MAGIC, None, ALU.subtract))
            link(dve.scalar_tensor_tensor(out=er[:, :], in0=ek[:, :], scalar=-LN2_HI, in1=sl[:, :], op0=ALU.mult, op1=ALU.add))
            link(dve.scalar_tensor_tensor(out=er[:, :], in0=ek[:, :], scalar=-LN2_LO, in1=er[:, :], op0=ALU.mult, op1=ALU.add))
            link(dve.tensor_scalar(ep[:, :], er[:, :], TAYLOR[0], None, ALU.mult))
            for coef in TAYLOR[1:]:
                link(dve.scalar_tensor_tensor(out=ep[:, :], in0=ep[:, :], scalar=coef, in1=er[:, :], op0=ALU.add, op1=ALU.mult))
            link(dve.tensor_scalar(ep[:, :], ep[:, :], 1.0, None, ALU.add))
            link(dve.tensor_scalar(ek[:, :], ek[:, :], 127.0, 8388608.0, ALU.add, ALU.mult))
            link(dve.tensor_copy(e2i[:, :], ek[:, :]))
            link(dve.tensor_tensor(gscale[:, :], ep[:, :], e2i[:, :].bitcast(F32), ALU.mult))
            link(dve.reciprocal(grec[:, :], gscale[:, :]))
            for ob in range(KI):
                rows = qv[:, ob * D:(ob + 1) * D]
                dve.wait_ge(lora_done, ob + 1)
                dve.scalar_tensor_tensor(out=rows, in0=bank[6 + ob % 2][:, :], scalar=LORA_SCALE, in1=rows,
                                         op0=ALU.mult, op1=ALU.add).then_inc(lora_used, 1)
                dve.wait_ge(lora_used, ob + 1)
                v = rows.rearrange("p (g n) -> p g n", g=G)
                link(dve.tensor_tensor(v, v, grec[:, ob * G:(ob + 1) * G].unsqueeze(2).broadcast_to([P, G, P]), ALU.mult))
            link(dve.tensor_scalar(qf[:, :], qv[:, :], 0.0, cb[:, 0:1], ALU.mult, ALU.add))

            dve.wait_ge(ld_res, 16)
            for i in range(KI):
                dve.tensor_scalar(xr[:, i, :], xr[:, i, :], bo_sb[:, i:i + 1], None, ALU.add).then_inc(res_ready, 1)

            def quantise(u, half, t):
                cols = slice(half * 1024, (half + 1) * 1024)
                if not isinstance(u, int) or u >= 1:
                    dve.wait_ge(quant_sum, u)
                dve.tensor_scalar(qm[:, :], qv[:, cols], thr[:, bass.ds(t + 1, 1)], step[:, bass.ds(t, 1)],
                                  ALU.is_gt, ALU.mult).then_inc(quant_mask, 1)
                dve.wait_ge(quant_mask, u + 1)
                dve.tensor_tensor(qf[:, cols], qf[:, cols], qm[:, :], ALU.add).then_inc(quant_sum, 1)

            def keep_scores(s, r, spill_count):
                hs, n = (r // NCH) % 2, r % NCH
                dve.wait_ge(scores_done, s + 1)
                if n == 0 and spill_count is not None:
                    dve.wait_ge(spilled[hs], spill_count)
                for j in range(NB):
                    rows = slice(j * C, (j + 1) * C)
                    src = bank[4 + r % 2][rows, :].rearrange("p (t n) -> p t n", t=TC)[:, :, j * C:(j + 1) * C]
                    dst = stage[rows, hs, n * TC * C:(n + 1) * TC * C].rearrange("p (t k) -> p t k", t=TC)
                    ins = dve.tensor_copy(dst, src)
                ins.then_inc(scores_kept, 1)

            units = 0
            for s in range(PRO_A):
                hh = s // NCH
                keep_scores(s, s % 8, 16 * (hh // 2) if hh >= 2 else None)
                for _ in range(2 if s >= PRO_A - (UNITS_PRO - PRO_A) else 1):
                    quantise(units, units % 2, units // 2)
                    units += 1
            with dve.Fori(0, LOOP_A) as i:
                for r in range(8):
                    keep_scores(8 * i + (PRO_A + r), (PRO_A + r) % 8, 16 * i + (16 + 16 * (r // NCH)))
                    quantise(8 * i + (UNITS_PRO + r), r % 2, dve.snap(4 * i + (UNITS_PRO // 2 + r // 2)))
            n_units = 2 * (NCODE - 1)
            for s in range(STEPS_A - NCH, STEPS_A):
                keep_scores(s, s % 8, 16 * (s // NCH // 2))
                if s == STEPS_A - 4:
                    dve.wait_ge(quant_sum, n_units)
                    link(dve.tensor_tensor(qf[:, :], qf[:, :], qv[:, :], ALU.subtract))
                    link(dve.tensor_tensor(qf[:, :], qf[:, :], qv[:, :], ALU.add))
                if s == STEPS_A - 3:
                    v = qf[:, :].rearrange("p (m n) -> p m n", n=P)
                    link(dve.tensor_tensor(v, v, gscale[:, :].unsqueeze(2).broadcast_to([P, KI * G, P]), ALU.mult))
                if s >= STEPS_A - 2:
                    for ob in range(2 * (s - STEPS_A + 2), 2 * (s - STEPS_A + 2) + 2):
                        rows = qf[:, ob * D:(ob + 1) * D]
                        dve.wait_ge(lora_done, KI + ob + 1)
                        dve.scalar_tensor_tensor(out=rows, in0=bank[6 + ob % 2][:, :], scalar=LORA_SCALE, in1=rows,
                                                 op0=ALU.mult, op1=ALU.add).then_inc(lora_used, 1)

            dve.wait_ge(stat_done, 1)
            dve.tensor_scalar(qv1[:, :], bank[4][:, 0:NT], 1.0 / INNER, EPS, ALU.mult, ALU.add).then_inc(var_ready, 1)
            for j in range(NB):
                rows = slice(j * C, (j + 1) * C)
                for c in range(NCH):
                    src = bank[c][rows, :].rearrange("p (t n) -> p t n", t=TC)[:, :, j * C:(j + 1) * C]
                    dst = kv[rows, c * TC * C:(c + 1) * TC * C].rearrange("p (t k) -> p t k", t=TC)
                    ins = dve.tensor_scalar(dst, src, 1.0 / INNER, EPS, ALU.mult, ALU.add)
            ins.then_inc(var_ready, 1)
            dve.wait_ge(std_ready, 2)
            for a, y, z in ((qv1, qn, qn2), (kv, kn, kn2)):
                link(dve.reciprocal(y[:, :], y[:, :]))
                link(dve.tensor_tensor(z[:, :], y[:, :], y[:, :], ALU.mult))
                link(dve.scalar_tensor_tensor(out=z[:, :], in0=z[:, :], scalar=-0.5, in1=a[:, :], op0=ALU.mult, op1=ALU.mult))
                link(dve.scalar_tensor_tensor(out=y[:, :], in0=z[:, :], scalar=1.5, in1=y[:, :], op0=ALU.add, op1=ALU.mult))
            link(dve.tensor_scalar(qn[:, :], qn[:, :], SCORE_SCALE, None, ALU.mult))
            dve.tensor_tensor(rqk[:, :].rearrange("p (t k) -> p t k", t=NT), kn[:, :].rearrange("p (t k) -> p t k", t=NT),
                              qn[:, :].unsqueeze(2).broadcast_to([P, NT, C]), ALU.mult).then_inc(rqk_ready, 1)

            def shift(q, qr):
                v = sc[:, qr % 2, :].rearrange("p (m k) -> p m k", k=C)
                dve.wait_ge(sm_scaled, q + 1)
                dve.tensor_reduce(mx[:, :], v, AX, ALU.max).then_inc(sm_max, 1)
                dve.wait_ge(sm_max, q + 1)
                dve.tensor_tensor(v, v, mx[:, :].unsqueeze(2).broadcast_to([P, 2 * NT, C]), ALU.subtract)\
                   .then_inc(sm_shift, 1)

            def invert(q, qr):
                v = sc[:, qr % 2, :].rearrange("p (m k) -> p m k", k=C)
                dve.wait_ge(sm_exp, q + 1)
                dve.tensor_reduce(rsum[:, :], v, AX, ALU.add).then_inc(sm_sum, 1)
                dve.wait_ge(sm_sum, q + 1)
                dve.reciprocal(rinv[:, :], rsum[:, :]).then_inc(sm_rinv, 1)

            def transpose_p(g, r, pair_count):
                if r % NCH == 0:
                    dve.wait_ge(p_ready, pair_count)
                if not isinstance(g, int) or g >= 2:
                    dve.wait_ge(pv_done, 2 * g - 2)
                n = r % NCH
                for j in range(NB):
                    rows = slice(j * C, (j + 1) * C)
                    src = sc[rows, (r // NCH) % 2, :].rearrange("p (h t k) -> p h t k", h=2, t=NT)[:, :, n * TC:(n + 1) * TC, :]
                    dst = pt[rows, r % 2, :, :, j * C:(j + 1) * C]
                    ins = dve.transpose(dst, src)
                ins.then_inc(pt_ready, 1)

            def out_lo(g, r, h):
                dve.wait_ge(o_hi, 2 * g + (h + 1))
                if h == 0 and (not isinstance(g, int) or g >= 2):
                    dve.wait_ge(wo_done, 4 * g - 4)
                dve.scalar_tensor_tensor(out=ot_lo[:, r % 2, h, :], in0=bank[2 + h][:, :], scalar=bvp[:, (r // NCH) % 2, h:h + 1],
                                         in1=ot_hi[:, r % 2, h, :].bitcast(F32), op0=ALU.add, op1=ALU.subtract)\
                   .then_inc(o_lo, 1)

            def add_out(g, r):
                n = r % NCH
                for i in range(KI):
                    dve.wait_ge(wo_done, 4 * g + (i + 1))
                    if not isinstance(g, int) or g >= 4:
                        dve.wait_ge(wo_added, 4 * g + (i - 15))
                    a = xr[:, i, n * CH:(n + 1) * CH]
                    dve.tensor_tensor(a, bank[4 + i][:, :], a, ALU.add).then_inc(wo_added, 1)

            dve.wait_ge(res_ready, KI)
            shift(0, 0)
            invert(0, 0)
            dve.wait_ge(pt_zero, 1)

            def step_b(g, r, pair, last=False):
                static = isinstance(g, int)
                if not static or g >= 1:
                    out_lo(g - 1, r + 7, 0)
                    out_lo(g - 1, r + 7, 1)
                transpose_p(g, r, pair)
                if not last:
                    if r % NCH == 1:
                        shift(pair, r // NCH + 1)
                    if r % NCH == 2:
                        invert(pair, r // NCH + 1)
                if not static or g >= 2:
                    add_out(g - 2, r + 6)

            for g in range(PRO_B):
                step_b(g, g, g // NCH + 1)
            with dve.Fori(0, LOOP_B) as i:
                for r in range(8):
                    step_b(8 * i + (PRO_B + r), r, 2 * i + (3 + r // NCH))
            for g in range(PRO_B + 8 * LOOP_B, STEPS_B):
                step_b(g, g % 8, g // NCH + 1, last=g // NCH == NP - 1)
            last = STEPS_B - 1
            out_lo(last, last % 8, 0)
            out_lo(last, last % 8, 1)
            add_out(last - 1, (last - 1) % 8)
            add_out(last, last % 8)

            for c in range(NCH):
                dve.wait_ge(rl_done, c + 1)
                for b2 in range(2):
                    link(dve.tensor_copy(rl[:, 2 * b2:2 * b2 + 2, :],
                                         bank[2 * c + b2][:, 0:2 * LR].rearrange("p (t n) -> p t n", t=2)))
                logit = rl[:, :, E_ * R_:LR]
                link(dve.tensor_tensor(lex, logit, br_sb[:, :].unsqueeze(1).broadcast_to([P, TC, E_]), ALU.add))
                link(dve.tensor_reduce(lmx[:, 0:TC], lex, AX, ALU.max))
                dve.tensor_tensor(lex, lex, lmx[:, 0:TC].unsqueeze(2).broadcast_to([P, TC, E_]), ALU.subtract)\
                   .then_inc(logit_shift, 1)
                dve.wait_ge(logit_exp, c + 1)
                link(dve.tensor_reduce(lsum[:, 0:TC], lex, AX, ALU.add))
                link(dve.reciprocal(linv[:, 0:TC], lsum[:, 0:TC]))
                link(dve.tensor_scalar(linv[:, 0:TC], linv[:, 0:TC], OUT_SCALE, None, ALU.mult))
                link(dve.tensor_tensor(lex, lex, linv[:, 0:TC].unsqueeze(2).broadcast_to([P, TC, E_]), ALU.mult))
                for t in range(TC):
                    ins = dve.tensor_tensor(low_s[:, t, :].rearrange("p (e r) -> p e r", e=E_),
                                            rl[:, t, 0:E_ * R_].rearrange("p (e r) -> p e r", e=E_),
                                            lex[:, t, :].unsqueeze(2).broadcast_to([P, E_, R_]), ALU.mult)
                ins.then_inc(low_scaled, 1)
                for i in range(KI):
                    n = c * KI + i
                    dve.wait_ge(fin_raw, n + 1)
                    a = xr[:, i, c * CH:(c + 1) * CH]
                    dve.tensor_tensor(a, bank[2 * c + 1 - i % 2][:, :], a, ALU.add).then_inc(fin_done, 1)


def kernel(**inputs):
    import numpy as np
    import concourse.bacc as bacc
    from concourse.bass_utils import run_bass_kernel_spmd

    a = {k: np.asarray(v) for k, v in inputs.items()}
    x = a["x"].reshape(NT, P, D)
    cols = lambda v: v.reshape(-1, P).T
    slices = lambda w: w.reshape(KI, P, -1).transpose(1, 0, 2)
    wq, wk = (a[f"L0_attn_W{n}"].reshape(KI, P, H, DH).transpose(2, 1, 0, 3) for n in "qk")
    wv = a["L0_attn_Wv"].reshape(KI, P, NP, 2 * DH).transpose(2, 1, 0, 3).reshape(NP, P, -1)
    wo = a["L0_attn_Wo"].reshape(NP, 2, DH, D).transpose(0, 2, 1, 3).reshape(NP, P, -1)
    laid = {
        "x_nat": x.transpose(1, 0, 2),
        "x_tr": slices(x.reshape(TOK, D).T),
        "cond_w": a["L0_cond_weights"].transpose(0, 2, 1),
        "cond_idx": np.broadcast_to(a["itok_B_0_15"], (S16, B)),
        "codebook": np.broadcast_to(a["condB_codebook"], (P, NCODE)),
        "wqk": np.concatenate([wq, wk], axis=2).reshape(H, P, -1),
        "wvo": np.concatenate([wv, wo], axis=2),
        "vecs": np.stack([cols(a[f"L0_attn_{n}"]) for n in ("bq", "bk", "bv", "gq", "gk")], axis=2),
        "bo": cols(a["L0_attn_bo"]),
        "w2": slices(a["L0_cond2_weight"]).reshape(P, -1),
        "scale_log": slices(a["L0_cond2_scale_log"].reshape(D, G)).reshape(P, -1),
        "lora_a": a["L0_cond2_lora_A"],
        "lora_bt": a["L0_cond2_lora_B"].T,
        "awr": slices(np.concatenate([a["L0_ffn_A"].reshape(E_ * R_, D).T, a["L0_ffn_Wr"].T], axis=1)),
        "bmat": a["L0_ffn_B"].transpose(0, 2, 1).reshape(E_ * R_, D),
        "br": np.broadcast_to(a["L0_ffn_br"], (P, E_)),
    }
    nc = bacc.Bacc("TRN2", target_bir_lowering=False, num_devices=1)
    arrays, args = {}, []
    for name, v in laid.items():
        v = np.ascontiguousarray(v)
        arrays[f"in_{name}"] = v
        args.append(nc.dram_tensor(f"in_{name}", v.shape, mybir.dt.from_np(v.dtype), kind="ExternalInput").ap())
    out = nc.dram_tensor("out_t", (P, KI, TOK), F32, kind="ExternalOutput").ap()
    build(nc, *args, out)
    r = run_bass_kernel_spmd(nc, [arrays], core_ids=[0])
    got = r.results[0]["out_t"]
    return got.transpose(1, 0, 2).reshape(D, TOK).T.reshape(B, C, D)
```

```python
from contextlib import ExitStack

import concourse.bass as bass
from concourse import mybir

F32 = mybir.dt.float32
F32R = mybir.dt.float32r
I32 = mybir.dt.int32
ALU = mybir.AluOpType
ACT = mybir.ActivationFunctionType
AX = mybir.AxisListType.X

P = 128
B, C, D = 64, 32, 512
KI = D // P
TOK = B * C
NT = TOK // P
NB = P // C
NCH = 4
TC = NT // NCH
CH = TC * P
H = 32
DH = 128
INNER = H * DH
S16 = 16
NP = H // 2
EPS = 1e-6
SCORE_SCALE = 1.0 / DH ** 0.5
G = 4
RANK = 64
LORA_SCALE = 32.0 / RANK
NCODE = 64
E_ = 8
R_ = 16
LR = E_ * R_ + E_
OUT_SCALE = E_ * (32.0 / R_)
BIG = 3.0e38
MAGIC = 12582912.0
LOG2E = 1.4426950408889634
LN2_HI, LN2_LO = 0.693359375, -2.12194440e-4
TAYLOR = [1 / 5040, 1 / 720, 1 / 120, 1 / 24, 1 / 6, 1 / 2, 1.0]

STEPS_A = H * NCH
PRO_A, LOOP_A = 12, 14
STEPS_B = NP * NCH
PRO_B, LOOP_B = 8, 6
FIRST = [(0, TC), (TC, 2 * TC), (2 * TC, NT)]
UNITS_PRO = 14


def build(nc, x_nat, x_tr, cond_w, cond_idx, codebook, wqk, wvo, vecs, bo, w2, scale_log,
          lora_a, lora_bt, awr, bmat, br, out_t):
    spill = nc.dram_tensor("score_spill", (H, P, NT * C), F32, kind="Internal").ap()

    with ExitStack() as ctx:
        def sb(name, shape, dt=F32):
            return ctx.enter_context(nc.sbuf_tensor(name, shape, dt))

        def sem(name):
            return ctx.enter_context(nc.semaphore(name))

        xc_hi = sb("xc_hi", [P, KI, TOK], F32R)
        xc_lo = sb("xc_lo", [P, KI, TOK], F32R)
        xres = sb("xres", [P, KI * TOK])
        w_raw = sb("w_raw", [P, 2, 1024])
        vec = sb("vec", [P, H, 5])
        hv = sb("hv", [P, 2, 5])
        bvp = sb("bvp", [P, 2, 2])
        bo_sb = sb("bo_sb", [P, KI])
        ident = sb("ident", [P, P])
        ones = sb("ones", [P, P])
        awr_sb = sb("awr_sb", [P, KI, LR])
        lowmat = sb("lowmat", [P, KI, LR])
        b_sb = sb("b_sb", [P, D])
        br_sb = sb("br_sb", [P, E_])
        rqk = sb("rqk", [P, NT * C])
        mx = sb("mx", [P, 2 * NT])
        rsum = sb("rsum", [P, 2 * NT])
        rinv = sb("rinv", [P, 2 * NT])

        x_in = xres[:, :].rearrange("p (t f) -> p t f", t=NT)
        xr = xres[:, :].rearrange("p (i n) -> p i n", i=KI)

        with ExitStack() as mem_a:
            def sba(name, shape, dt=F32):
                return mem_a.enter_context(nc.sbuf_tensor(name, shape, dt))
            mixw = sba("mixw", [P, NT, P])
            wa = sba("wa", [P, 2, 2, 1024], F32R)
            qk = sba("qk", [P, 2, 2, CH])
            sq = sba("sq", [P, 2, 2, CH])
            acc = sba("acc", [P, 2, TOK])
            stage = sba("stage", [P, 2, NT * C])
            qv = sba("qv", [P, KI * D])
            qf = sba("qf", [P, KI * D])
            qm = sba("qm", [P, 1024])
            cw = qm[0:S16, :]
            idx_i = sba("idx_i", [S16, B], I32)
            idx_f = sba("idx_f", [S16, B])
            row_i = sba("row_i", [S16, 1], I32)
            row_f = sba("row_f", [S16, 1])
            onehot = sba("onehot", [S16, B])
            cb = sba("cb", [P, NCODE])
            cbmax = sba("cbmax", [P, 2])
            thr = sba("thr", [P, NCODE + 1])
            thr_t = sba("thr_t", [P, NCODE])
            step = sba("step", [P, NCODE])
            sl = sba("sl", [P, KI * G])
            ek = sba("ek", [P, KI * G])
            er = sba("er", [P, KI * G])
            ep = sba("ep", [P, KI * G])
            e2i = sba("e2i", [P, KI * G], I32)
            gscale = sba("gscale", [P, KI * G])
            grec = sba("grec", [P, KI * G])
            la = sba("la", [RANK, D])
            lbt = sba("lbt", [RANK, D])
            kv = sba("kv", [P, NT * C])
            kn = sba("kn", [P, NT * C])
            kn2 = sba("kn2", [P, NT * C])
            qv1 = sba("qv1", [P, NT])
            qn = sba("qn", [P, NT])
            qn2 = sba("qn2", [P, NT])
            update = mixw[:, :, :].rearrange("p t n -> p (t n)")
        wv0 = sb("wv0", [P, 2, 1024], F32R)
        wv1 = sb("wv1", [P, 2, 1024], F32R)
        vb = sb("vb", [P, 2, TC, 2 * DH])
        wo0 = sb("wo0", [P, 2, 1024], F32R)
        wo1 = sb("wo1", [P, 2, 1024], F32R)
        sc = sb("sc", [P, 2, 2 * NT * C])
        pt = sb("pt", [P, 2, 2, TC, P])
        ot_hi = sb("ot_hi", [P, 2, 2, CH], F32R)
        ot_lo = sb("ot_lo", [P, 2, 2, CH], F32R)
        wv, wo = (wv0, wv1), (wo0, wo1)
        rl = vb[:, :, :, :].rearrange("p a t n -> p (a t n)")[:, 0:TC * LR].rearrange("p (t n) -> p t n", t=TC)
        sc_flat = sc[:, :, :].rearrange("p a n -> p (a n)")
        low_s = sc_flat[:, 0:CH].rearrange("p (t n) -> p t n", t=TC)
        low_t = [sc_flat[:, (1 + a) * CH:(2 + a) * CH] for a in range(2)]
        lmx = sc_flat[:, 3 * CH:3 * CH + 8]
        lsum = sc_flat[:, 3 * CH + 8:3 * CH + 16]
        linv = sc_flat[:, 3 * CH + 16:3 * CH + 24]
        lex = sc_flat[:, 3 * CH + 32:3 * CH + 64].rearrange("p (t e) -> p t e", t=TC)

        bank = [ctx.enter_context(nc.psum_tensor(f"bank{i}", [P, 512], F32)) for i in range(8)]

        ld_cond = sem("ld_cond")
        ld_x = [sem(f"ld_x{c}") for c in range(NCH)]
        ld_vec = sem("ld_vec")
        ld_code = sem("ld_code")
        ld_quant = sem("ld_quant")
        ld_res = sem("ld_res")
        iota_done = sem("iota_done")
        const_done = sem("const_done")
        mix_zero = sem("mix_zero")
        mix_raw = sem("mix_raw")
        mix_done = sem("mix_done")
        onehot_done = sem("onehot_done")
        lora_done = sem("lora_done")
        lora_used = sem("lora_used")
        w_eff_done = sem("w_eff_done")
        xc_raw = sem("xc_raw")
        xc_hi_done = sem("xc_hi_done")
        xc_lo_done = sem("xc_lo_done")
        vec_ready = sem("vec_ready")
        hv_ready = sem("hv_ready")
        bvp_ready = sem("bvp_ready")
        chain = sem("chain")
        wqk_loaded = [sem("wqk_loaded0"), sem("wqk_loaded1")]
        wqk_hi = sem("wqk_hi")
        wqk_lo = sem("wqk_lo")
        proj_done = sem("proj_done")
        qk_copied = sem("qk_copied")
        sq_ready = sem("sq_ready")
        acc_zero = sem("acc_zero")
        acc_done = sem("acc_done")
        scores_done = sem("scores_done")
        scores_kept = sem("scores_kept")
        spilled = [sem("spilled0"), sem("spilled1")]
        quant_mask = sem("quant_mask")
        quant_sum = sem("quant_sum")
        low_raw = sem("low_raw")
        low_ready = sem("low_ready")
        stat_done = sem("stat_done")
        var_ready = sem("var_ready")
        std_ready = sem("std_ready")
        rqk_ready = sem("rqk_ready")
        wvo_loaded = sem("wvo_loaded")
        wvo_hi = sem("wvo_hi")
        wvo_lo = sem("wvo_lo")
        res_ready = sem("res_ready")
        pt_zero = sem("pt_zero")
        sc_loaded = [sem("sc_loaded0"), sem("sc_loaded1")]
        first_shifted = sem("first_shifted")
        first_exp = sem("first_exp")
        sm_scaled = sem("sm_scaled")
        sm_max = sem("sm_max")
        sm_shift = sem("sm_shift")
        sm_exp = sem("sm_exp")
        sm_sum = sem("sm_sum")
        sm_rinv = sem("sm_rinv")
        p_ready = sem("p_ready")
        pt_ready = sem("pt_ready")
        v_done = sem("v_done")
        v_kept = sem("v_kept")
        pv_done = sem("pv_done")
        o_hi = sem("o_hi")
        o_lo = sem("o_lo")
        wo_done = sem("wo_done")
        wo_added = sem("wo_added")
        rl_done = sem("rl_done")
        rl_kept = sem("rl_kept")
        logit_shift = sem("logit_shift")
        logit_exp = sem("logit_exp")
        low_scaled = sem("low_scaled")
        lowt_raw = sem("lowt_raw")
        lowt_done = sem("lowt_done")
        fin_raw = sem("fin_raw")
        fin_done = sem("fin_done")
        stored = sem("stored")

        def scores_view(ap):
            return ap.rearrange("p (h t k) -> p h t k", h=2, t=NT)

        def mix_bank(n):
            return 4 + n % 4 if n < 2 * KI else 6 + n % 2

        mix_after = {(0, 0): [8], (0, 1): [9], (1, 0): [10, 11], (1, 1): [12, 13], (2, 0): [14, 15]}

        def lowt_bank(c):
            return [bank[2], bank[4], bank[5], bank[4]][c]

        def fin_bank(c, i):
            return bank[2 + i % 2] if c == 0 else bank[[2, 3, 6, 7][i]]

        def mix_block(q, j):
            src = bank[0][q * C:(q + 1) * C, :].rearrange("p (m t j) -> p j t m", m=C // NB, j=NB)[:, j]
            return mixw[j * C:(j + 1) * C, :, j * C + q:(j + 1) * C:NB], src

        block = ctx.enter_context(nc.Block())

        @block.sync
        def _(sp):
            def load_x(c):
                sp.dma_start(x_in[:, c * TC:(c + 1) * TC, :], x_nat[:, c * TC:(c + 1) * TC, :]).then_inc(ld_x[c], 16)

            sp.dma_start(cw, cond_w).then_inc(ld_cond, 16)
            load_x(0)
            sp.dma_start(w_raw[:, 0, :], wqk[0]).then_inc(wqk_loaded[0], 16)
            load_x(1)
            sp.dma_start(w_raw[:, 1, :], wqk[1]).then_inc(wqk_loaded[1], 16)
            load_x(2)
            load_x(3)
            for dst, src in ((la[:, :], lora_a), (lbt[:, :], lora_bt), (qv[:, :], w2), (awr_sb[:, :, :], awr),
                             (b_sb[:, :], bmat), (br_sb[:, :], br), (bo_sb[:, :], bo)):
                sp.dma_start(dst, src).then_inc(ld_quant, 16)
            sp.wait_ge(xc_raw, NT)
            sp.dma_start(xr, x_tr).then_inc(ld_res, 16)

            def load_head(h, hr, split_count):
                sp.wait_ge(wqk_lo, split_count)
                sp.dma_start(w_raw[:, hr % 2, :], wqk[h]).then_inc(wqk_loaded[hr % 2], 16)

            def spill_head(h, hr, kept_count):
                sp.wait_ge(scores_kept, kept_count)
                sp.dma_start(spill[h], stage[:, hr % 2, :]).then_inc(spilled[hr % 2], 16)

            for h in range(3):
                load_head(h + 2, h, h + 1)
                spill_head(h, h, 4 * h + 4)
            with sp.Fori(0, LOOP_A - 1) as i:
                for r in range(2):
                    load = sp.snap(2 * i + (5 + r))
                    store = sp.snap(2 * i + (3 + r))
                    split = sp.snap(2 * i + (4 + r))
                    kept = sp.snap(8 * i + (16 + 4 * r))
                    sp.wait_ge(wqk_lo, split)
                    sp.dma_start(w_raw[:, (1 + r) % 2, :], wqk[bass.ds(load, 1)].rearrange("a p n -> (a p) n"))\
                      .then_inc(wqk_loaded[(1 + r) % 2], 16)
                    sp.wait_ge(scores_kept, kept)
                    sp.dma_start(spill[bass.ds(store, 1)].rearrange("a p n -> (a p) n"), stage[:, (1 + r) % 2, :])\
                      .then_inc(spilled[(1 + r) % 2], 16)
            load_head(H - 1, H - 1, H - 2)
            spill_head(H - 3, H - 3, 4 * (H - 2))
            w_all = w_raw[:, :, :].rearrange("p a n -> p (a n)")
            sp.wait_ge(wqk_lo, H)
            sp.dma_start(w_all, wvo[0]).then_inc(wvo_loaded, 16)
            spill_head(H - 2, H - 2, 4 * (H - 1))
            spill_head(H - 1, H - 1, 4 * H)

            sp.wait_ge(spilled[0], 16 * NP)
            sp.wait_ge(spilled[1], 16 * NP)

            def load_scores(q):
                if q >= 2:
                    sp.wait_ge(pt_ready, 4 * q - 4)
                sp.dma_start(sc[:, q % 2, :].rearrange("p (a n) -> p a n", a=2),
                             spill[2 * q:2 * q + 2].rearrange("a p n -> p a n")).then_inc(sc_loaded[q % 2], 16)

            def load_wvo(p):
                sp.wait_ge(wvo_lo, 2 * p)
                sp.dma_start(w_all, wvo[p]).then_inc(wvo_loaded, 16)

            sp.wait_ge(stat_done, 1)
            load_scores(0)
            load_wvo(1)
            load_scores(1)
            load_wvo(2)
            load_scores(2)
            load_wvo(3)
            load_scores(3)
            with sp.Fori(0, LOOP_B) as i:
                for r in range(2):
                    pair = sp.snap(2 * i + (4 + r))
                    half = sp.snap(4 * i + (8 + 2 * r))
                    parts = sp.snap(4 * i + (8 + 2 * r))
                    used = sp.snap(8 * i + (12 + 4 * r))
                    sp.wait_ge(wvo_lo, parts)
                    sp.dma_start(w_all, wvo[bass.ds(pair, 1)].rearrange("a p n -> (a p) n")).then_inc(wvo_loaded, 16)
                    sp.wait_ge(pt_ready, used)
                    sp.dma_start(sc[:, r, :].rearrange("p (a n) -> p a n", a=2),
                                 spill[bass.ds(half, 2)].rearrange("a p n -> p a n")).then_inc(sc_loaded[r], 16)

            for c in range(NCH):
                for i in range(KI):
                    n = c * KI + i
                    sp.wait_ge(fin_done, n + 1)
                    sp.dma_start(out_t[:, i, c * CH:(c + 1) * CH], xr[:, i, c * CH:(c + 1) * CH]).then_inc(stored, 16)
            sp.wait_ge(stored, 16 * NCH * KI)

        @block.tensor
        def _(pe):
            pe.wait_ge(ld_cond, 32)
            pe.wait_ge(onehot_done, 1)
            for m in range(C // NB):
                ins = pe.matmul(bank[0][:, m * B:(m + 1) * B], cw[:, m * P:(m + 1) * P], onehot[:, :],
                                start=True, stop=True)
            ins.then_inc(mix_raw, 1)

            def mix(n):
                c, i = n // KI, n % KI
                if i == 0:
                    pe.wait_ge(ld_x[c], 16)
                if n >= 4:
                    pe.wait_ge(xc_lo_done, n - 3 if n < 8 else n - 1)
                for t in range(TC):
                    ins = pe.matmul(bank[mix_bank(n)][:, t * P:(t + 1) * P], x_in[:, c * TC + t, i * P:(i + 1) * P],
                                    mixw[:, c * TC + t, :], start=True, stop=True)
                ins.then_inc(xc_raw, 1)

            def lora(ob):
                pe.matmul(bank[6 + ob % 2][:, :], lbt[:, ob * P:(ob + 1) * P], la[:, :],
                          start=True, stop=True).then_inc(lora_done, 1)

            pe.wait_ge(mix_done, NB * NB)
            for n in range(2 * KI):
                mix(n)

            def project(s, r, kind):
                u = 2 * r + kind
                hs, n = (r // NCH) % 2, r % NCH
                dst = bank[u % 4][:, :]
                k = 0
                for i in range(KI):
                    col = kind * 512 + i * P
                    for wpart, xpart in ((0, xc_hi), (0, xc_lo), (1, xc_hi)):
                        ins = pe.matmul(dst, wa[:, hs, wpart, col:col + P], xpart[:, i, n * CH:(n + 1) * CH],
                                        start=(k == 0), stop=(k == 11))
                        k += 1
                ins.then_inc(proj_done, 1)

            def scores(s, r):
                for t in range(TC):
                    ins = pe.matmul(bank[4 + r % 2][:, t * P:(t + 1) * P], qk[:, r % 2, 0, t * P:(t + 1) * P],
                                    qk[:, r % 2, 1, t * P:(t + 1) * P], start=True, stop=True)
                ins.then_inc(scores_done, 1)

            def step_a(s, r, first=0):
                if r % NCH == 0:
                    if isinstance(s, int):
                        pe.wait_ge(wqk_lo, s // NCH + 1)
                    else:
                        pe.wait_ge(wqk_lo, first)
                if not isinstance(s, int) or s >= 2:
                    pe.wait_ge(sq_ready, 2 * s - 3)
                if isinstance(s, int) and s < NCH:
                    pe.wait_ge(xc_lo_done, KI * (s + 1))
                project(s, r, 0)
                if isinstance(s, int):
                    for n in mix_after.get((s, 0), []):
                        mix(n)
                if not isinstance(s, int) or s >= 1:
                    scores_when(s - 1, r + 7)
                if not isinstance(s, int) or s >= 2:
                    pe.wait_ge(sq_ready, 2 * s - 2)
                project(s, r, 1)
                if isinstance(s, int):
                    for n in mix_after.get((s, 1), []):
                        mix(n)

            def scores_when(s, r):
                pe.wait_ge(qk_copied, 2 * s + 2)
                if not isinstance(s, int) or s >= 2:
                    pe.wait_ge(scores_kept, s - 1)
                scores(s, r)

            for s in range(PRO_A):
                step_a(s, s % 8)
                if s == 3:
                    pe.wait_ge(ld_quant, 16 * 7)
                    pe.wait_ge(xc_lo_done, NCH * KI)
                    lora(0)
                    lora(1)
                if s == 5:
                    for ob in (2, 3):
                        pe.wait_ge(lora_used, ob - 1)
                        lora(ob)
            with pe.Fori(0, LOOP_A) as i:
                for r in range(8):
                    step_a(8 * i + (PRO_A + r), (PRO_A + r) % 8, 2 * i + (4 + r // NCH))
            for s in range(STEPS_A - NCH, STEPS_A):
                step_a(s, s % 8)

            def norm_sums():
                pe.wait_ge(acc_done, 2 * STEPS_A)
                pe.wait_ge(scores_kept, STEPS_A - 1)
                for t in range(NT):
                    pe.matmul(bank[4][:, t:t + 1], acc[:, 0, t * P:(t + 1) * P], ones[:, 0:1], start=True, stop=True)
                pe.wait_ge(scores_kept, STEPS_A)
                for j in range(NB):
                    keys = acc[:, 1, :].rearrange("p (t n) -> p t n", t=NT)[:, :, j * C:(j + 1) * C]
                    ins = pe.matmul(bank[5][j * C:(j + 1) * C, :].rearrange("p (t k) -> p t k", t=NT), ones[:, 0:C], keys,
                                    start=True, stop=True)
                ins.then_inc(stat_done, 1)

            def low_product():
                pe.wait_ge(w_eff_done, 1)
                for i in range(KI):
                    for ob in range(KI):
                        ins = pe.matmul(bank[6 + i // 2][:, (i % 2) * LR:(i % 2 + 1) * LR],
                                        qf[:, ob * D + i * P:ob * D + (i + 1) * P], awr_sb[:, ob, :],
                                        start=(ob == 0), stop=(ob == KI - 1))
                ins.then_inc(low_raw, 1)

            def v_half(g, r, half):
                slot, n = (r // NCH) % 2, r % NCH
                if not isinstance(g, int) or g >= 1:
                    pe.wait_ge(v_kept, 2 * g + (half - 1))
                for t in range(2):
                    tile = n * TC + half * 2 + t
                    k = 0
                    for i in range(KI):
                        for xpart, wpart in ((xc_hi, 0), (xc_hi, 1), (xc_lo, 0)):
                            ins = pe.matmul(bank[half][:, t * 256:(t + 1) * 256], xpart[:, i, tile * P:(tile + 1) * P],
                                            wv[slot][:, wpart, i * 256:(i + 1) * 256], start=(k == 0), stop=(k == 11))
                            k += 1
                ins.then_inc(v_done, 1)

            def pv(g, r, h):
                if h == 0:
                    pe.wait_ge(v_kept, 2 * g + 2)
                    pe.wait_ge(pt_ready, g + 1)
                if not isinstance(g, int) or g >= 1:
                    pe.wait_ge(o_lo, 2 * g + (h - 1))
                for t in range(TC):
                    ins = pe.matmul(bank[2 + h][:, t * P:(t + 1) * P], vb[:, r % 2, t, h * DH:(h + 1) * DH],
                                    pt[:, r % 2, h, t, :], start=True, stop=True)
                ins.then_inc(pv_done, 1)

            def project_out(g, r):
                slot = (r // NCH) % 2
                pe.wait_ge(o_lo, 2 * g + 2)
                for i in range(KI):
                    if not isinstance(g, int) or g >= 1:
                        pe.wait_ge(wo_added, 4 * g + (i - 3))
                    k = 0
                    for h in range(2):
                        col = h * D + i * P
                        for wpart, opart in ((0, ot_hi), (0, ot_lo), (1, ot_hi)):
                            ins = pe.matmul(bank[4 + i][:, :], wo[slot][:, wpart, col:col + P],
                                            opart[:, r % 2, h, :], start=(k == 0), stop=(k == 5))
                            k += 1
                    ins.then_inc(wo_done, 1)

            def step_b(g, r, wv_parts=None, wo_parts=None):
                static = isinstance(g, int)
                if r % NCH == 0:
                    pe.wait_ge(wvo_lo, 2 * (g // NCH) + 1 if static else wv_parts)
                v_half(g, r, 0)
                if not static or g >= 1:
                    pv(g - 1, r + 7, 0)
                v_half(g, r, 1)
                if not static or g >= 1:
                    pv(g - 1, r + 7, 1)
                if r % NCH == 2 and (not static or g >= 2):
                    pe.wait_ge(wvo_lo, 2 * ((g - 2) // NCH) + 2 if static else wo_parts)
                if not static or g >= 2:
                    project_out(g - 2, r + 6)

            low_product()
            scores_when(STEPS_A - 1, (STEPS_A - 1) % 8)
            norm_sums()
            pe.wait_ge(sq_ready, 2 * STEPS_A)
            pe.wait_ge(wvo_lo, 1)
            v_half(0, 0, 0)
            v_half(0, 0, 1)
            v_half(1, 1, 0)
            v_half(1, 1, 1)
            pv(0, 0, 0)
            pv(0, 0, 1)
            pe.wait_ge(low_ready, 2)
            pe.wait_ge(var_ready, 1 + len(FIRST))
            for g in range(2, PRO_B):
                step_b(g, g)
            with pe.Fori(0, LOOP_B) as i:
                for r in range(8):
                    step_b(8 * i + (PRO_B + r), r, 4 * i + (5 + 2 * (r // NCH)), 4 * i + (6 + 2 * (r // NCH)))
            for g in range(PRO_B + 8 * LOOP_B, STEPS_B):
                step_b(g, g % 8)
            last = STEPS_B - 1

            def low_rank(c):
                pe.wait_ge(wo_added, 4 * (STEPS_B - NCH + c + 1))
                if c >= 1:
                    pe.wait_ge(rl_kept, c)
                else:
                    pe.wait_ge(v_kept, 2 * STEPS_B)
                for t in range(TC):
                    for i in range(KI):
                        n = c * TC + t
                        ins = pe.matmul(bank[t // 2][:, (t % 2) * LR:(t % 2 + 1) * LR],
                                        xr[:, i, n * P:(n + 1) * P], lowmat[:, i, :], start=(i == 0), stop=(i == KI - 1))
                ins.then_inc(rl_done, 1)

            def transpose_low(c):
                pe.wait_ge(low_scaled, c + 1)
                if c == 0:
                    pe.wait_ge(o_lo, 2 * STEPS_B)
                elif c <= 2:
                    pe.wait_ge(wo_added, 4 * STEPS_B - 4 + c)
                else:
                    pe.wait_ge(lowt_done, c - 1)
                for t in range(TC):
                    ins = pe.transpose(lowt_bank(c)[:, t * P:(t + 1) * P], low_s[:, t, :], ident[:, :])
                ins.then_inc(lowt_raw, 1)

            def experts(c, half):
                pe.wait_ge(lowt_done, c + 1)
                for i in (2 * half, 2 * half + 1):
                    if c == 0:
                        if i >= 2:
                            pe.wait_ge(fin_done, i - 1)
                    elif c == 1:
                        pe.wait_ge(fin_done, KI)
                        pe.wait_ge(wo_added, 4 * STEPS_B)
                    else:
                        pe.wait_ge(fin_done, (c - 1) * KI + i + 1)
                    pe.matmul(fin_bank(c, i)[:, :], b_sb[:, i * P:(i + 1) * P], low_t[c % 2],
                              start=True, stop=True).then_inc(fin_raw, 1)

            low_rank(0)
            pv(last, last % 8, 0)
            pv(last, last % 8, 1)
            project_out(last - 1, (last - 1) % 8)
            transpose_low(0)
            low_rank(1)
            experts(0, 0)
            project_out(last, last % 8)
            transpose_low(1)
            experts(0, 1)
            low_rank(2)
            experts(1, 0)
            low_rank(3)
            transpose_low(2)
            experts(1, 1)
            experts(2, 0)
            transpose_low(3)
            experts(2, 1)
            experts(3, 0)
            experts(3, 1)

        @block.scalar
        def _(act):
            def wqk_part(h, hr, load_count, free_count):
                act.wait_ge(wqk_loaded[hr % 2], load_count)
                if free_count is not None:
                    act.wait_ge(proj_done, free_count)
                act.activation(wa[:, hr % 2, 0, :], w_raw[:, hr % 2, :], ACT.Copy).then_inc(wqk_hi, 1)

            act.dma_start(idx_i[:, :], cond_idx).then_inc(ld_cond, 16)
            act.dma_start(cb[:, :], codebook).then_inc(ld_code, 16)
            act.dma_start(sl[:, :], scale_log).then_inc(ld_code, 16)
            act.dma_start(vec[:, :, :], vecs).then_inc(ld_vec, 16)

            act.wait_ge(mix_zero, 1)
            act.wait_ge(mix_raw, 1)
            for q in (2, 3):
                for j in range(NB):
                    dst, src = mix_block(q, j)
                    act.activation(dst, src, ACT.Copy).then_inc(mix_done, 1)

            def mix_hi(n):
                c, i = n // KI, n % KI
                act.wait_ge(xc_raw, n + 1)
                act.activation(xc_hi[:, i, c * CH:(c + 1) * CH], bank[mix_bank(n)][:, :], ACT.Copy).then_inc(xc_hi_done, 1)

            wqk_part(0, 0, 16, None)
            for n in range(2 * KI):
                mix_hi(n)
            wqk_part(1, 1, 16, None)

            def step_a(s, r, h, load_count):
                static = isinstance(s, int)
                hs = (r // NCH) % 2
                if r % NCH == 0:
                    act.activation(hv[:, hs:hs + 1, :], vec[:, bass.ds(h, 1), :], ACT.Copy).then_inc(hv_ready, 1)
                    act.wait_ge(hv_ready, h + 1)
                for kind in range(2):
                    u = 2 * r + kind
                    act.wait_ge(proj_done, 2 * s + (1 + kind))
                    if kind == 0 and (not static or s >= 2):
                        act.wait_ge(scores_done, s - 1)
                    scale = hv[:, hs, 3:4] if kind == 0 else 1.0
                    bias = hv[:, hs, 4:5] if kind == 0 else hv[:, hs, 1:2]
                    act.activation(qk[:, r % 2, kind, :], bank[u % 4][:, :], ACT.Identity, bias=bias, scale=scale)\
                       .then_inc(qk_copied, 1)
                    if not static or s >= 2:
                        act.wait_ge(acc_done, 2 * s + (kind - 3))
                    act.activation(sq[:, r % 2, kind, :], bank[u % 4][:, :], ACT.Square,
                                   bias=hv[:, hs, kind:kind + 1], scale=1.0).then_inc(sq_ready, 1)
                    if static:
                        for n in mix_after.get((s, kind), []):
                            mix_hi(n)
                if r % NCH == 1 and not (static and s // NCH + 1 >= H):
                    if static:
                        hh = s // NCH + 1
                        if hh >= 2:
                            wqk_part(hh, hh, 16 * (hh // 2 + 1), 8 * (hh - 1))
                    else:
                        wqk_part(None, r // NCH + 1, load_count, 2 * s - 2)

            act.wait_ge(vec_ready, 2)
            for s in range(PRO_A):
                step_a(s, s % 8, s // NCH, None)
            with act.Fori(0, LOOP_A) as i:
                for r in range(8):
                    if r % NCH == 0:
                        hreg = act.snap(2 * i + (3 + r // NCH))
                    step_a(8 * i + (PRO_A + r), (PRO_A + r) % 8, hreg, 16 * i + 48)

            def wvo_part(r, part, load_count, free_sem, free_count):
                act.wait_ge(wvo_loaded, load_count)
                if free_sem is not None:
                    act.wait_ge(free_sem, free_count)
                act.activation((wv, wo)[part][r % 2][:, 0, :], w_raw[:, part, :], ACT.Copy).then_inc(wvo_hi, 1)

            for s in range(STEPS_A - NCH, STEPS_A):
                step_a(s, s % 8, s // NCH, None)
                if s == STEPS_A - 2:
                    wvo_part(0, 0, 16, w_eff_done, 1)
            def exps(q, qr):
                act.wait_ge(sm_shift, q)
                act.activation(sc[:, qr % 2, :], sc[:, qr % 2, :], ACT.Exp).then_inc(sm_exp, 1)

            def first_exps(part):
                t0, t1 = FIRST[part]
                act.wait_ge(first_shifted, part + 1)
                v = sc[:, 0, :].rearrange("p (h n) -> p h n", h=2)[:, :, t0 * C:t1 * C]
                act.activation(v, v, ACT.Exp).then_inc(first_exp, 1)

            def copy_v(g, r, half):
                act.wait_ge(v_done, 2 * g + (half + 1))
                if half == 0 and (not isinstance(g, int) or g >= 2):
                    act.wait_ge(pv_done, 2 * g - 2)
                act.activation(vb[:, r % 2, 2 * half:2 * half + 2, :],
                               bank[half][:, :].rearrange("p (t n) -> p t n", t=2), ACT.Copy).then_inc(v_kept, 1)

            def pair_bias(p, pr, head):
                act.activation(bvp[:, pr % 2, :], vec[:, bass.ds(head, 2), 2], ACT.Copy).then_inc(bvp_ready, 1)
                act.wait_ge(bvp_ready, p + 1)

            def out_hi(g, r, h):
                act.wait_ge(pv_done, 2 * g + (h + 1))
                if h == 0 and (not isinstance(g, int) or g >= 2):
                    act.wait_ge(wo_done, 4 * g - 4)
                act.activation(ot_hi[:, r % 2, h, :], bank[2 + h][:, :], ACT.Identity,
                               bias=bvp[:, (r // NCH) % 2, h:h + 1], scale=1.0).then_inc(o_hi, 1)

            def step_b(g, r, loaded, pair, head=None, last=False):
                static = isinstance(g, int)
                copy_v(g, r, 0)
                if not static or g >= 1:
                    out_hi(g - 1, r + 7, 0)
                copy_v(g, r, 1)
                if not static or g >= 1:
                    out_hi(g - 1, r + 7, 1)
                if r % NCH == 0:
                    pair_bias(pair - 1, r // NCH, head)
                if not last:
                    if r % NCH == 1:
                        wvo_part(r // NCH + 1, 0, loaded, v_done, 2 * g - 2) if (not static or g > 1) else \
                            wvo_part(r // NCH + 1, 0, loaded, None, None)
                        exps(pair, r // NCH + 1)
                    if r % NCH == 2:
                        wvo_part(r // NCH + 1, 1, loaded, wo_done, 4 * g - 8) if (not static or g > 2) else \
                            wvo_part(r // NCH + 1, 1, loaded, None, None)

            act.wait_ge(low_raw, 1)
            for b2 in range(2):
                act.activation(lowmat[:, 2 * b2:2 * b2 + 2, :], bank[6 + b2][:, 0:2 * LR].rearrange("p (i n) -> p i n", i=2),
                               ACT.Copy).then_inc(low_ready, 1)
            act.wait_ge(scores_done, STEPS_A)
            act.wait_ge(acc_done, 2 * STEPS_A)
            wvo_part(0, 1, 16, None, None)
            act.wait_ge(var_ready, 1)
            act.activation(qn[:, :], qv1[:, :], ACT.Sqrt).then_inc(std_ready, 1)
            for part, (t0, t1) in enumerate(FIRST):
                act.wait_ge(var_ready, part + 2)
                act.activation(kn[:, t0 * C:t1 * C], kv[:, t0 * C:t1 * C], ACT.Sqrt).then_inc(std_ready, 1)
            copy_v(0, 0, 0)
            first_exps(0)
            pair_bias(0, 0, 0)
            copy_v(0, 0, 1)
            copy_v(1, 1, 0)
            first_exps(1)
            copy_v(1, 1, 1)
            act.wait_ge(spilled[0], 16 * NP)
            act.wait_ge(spilled[1], 16 * NP)
            out_hi(0, 0, 0)
            out_hi(0, 0, 1)
            first_exps(2)
            wvo_part(1, 0, 32, None, None)
            for g in range(2, PRO_B):
                p = g // NCH
                step_b(g, g, 16 * (p + 2), p + 1, 2 * p)
                if g == 2:
                    exps(1, 1)
            with act.Fori(0, LOOP_B) as i:
                for r in range(8):
                    if r % NCH == 0:
                        head = act.snap(4 * i + (4 + 2 * (r // NCH)))
                    step_b(8 * i + (PRO_B + r), r, 32 * i + (64 + 16 * (r // NCH)), 2 * i + (3 + r // NCH), head)
            for g in range(PRO_B + 8 * LOOP_B, STEPS_B):
                p = g // NCH
                step_b(g, g % 8, 16 * (p + 2), p + 1, 2 * p, last=p == NP - 1)

            def expert_exp(c):
                act.wait_ge(logit_shift, c + 1)
                act.activation(lex, lex, ACT.Exp).then_inc(logit_exp, 1)

            def keep_lowt(c):
                act.wait_ge(lowt_raw, c + 1)
                act.activation(low_t[c % 2], lowt_bank(c)[:, :], ACT.Copy).then_inc(lowt_done, 1)

            expert_exp(0)
            out_hi(STEPS_B - 1, (STEPS_B - 1) % 8, 0)
            out_hi(STEPS_B - 1, (STEPS_B - 1) % 8, 1)
            for c in range(NCH):
                keep_lowt(c)
                if c + 1 < NCH:
                    expert_exp(c + 1)

        @block.gpsimd
        def _(pool):
            pool.iota(row_i[:, :], pattern=[[0, 1]], base=0, channel_multiplier=1).then_inc(iota_done, 1)
            pool.memset(mixw[:, :, :], 0.0).then_inc(mix_zero, 1)
            pool.memset(ones[:, :], 1.0).then_inc(const_done, 1)
            pool.memset(ident[:, :], 0.0).then_inc(const_done, 1)
            pool.wait_ge(const_done, 2)
            pool.affine_select(out=ident[:, :], in_=ident[:, :], compare_op=ALU.not_equal, fill=1.0,
                               base=0, pattern=[[-1, P]], channel_multiplier=1).then_inc(const_done, 1)
            pool.memset(acc[:, :, :], 0.0).then_inc(acc_zero, 1)
            pool.wait_ge(acc_zero, 1)

            def wqk_part(hr, count):
                pool.wait_ge(wqk_hi, count)
                pool.tensor_tensor(wa[:, hr % 2, 1, :], w_raw[:, hr % 2, :], wa[:, hr % 2, 0, :].bitcast(F32),
                                   ALU.subtract).then_inc(wqk_lo, 1)

            wqk_part(0, 1)
            wqk_part(1, 2)

            def step_a(s, r, part_count):
                static = isinstance(s, int)
                n = r % NCH
                for kind in range(2):
                    pool.wait_ge(sq_ready, 2 * s + (1 + kind))
                    if not static or s >= 4:
                        pool.wait_ge(acc_done, 2 * s + (kind - 7))
                    a = acc[:, kind, n * CH:(n + 1) * CH]
                    pool.tensor_tensor(a, a, sq[:, r % 2, kind, :], ALU.add).then_inc(acc_done, 1)
                if n == 1:
                    if static:
                        if 2 <= s // NCH + 1 < H:
                            wqk_part(s // NCH + 1, s // NCH + 2)
                    else:
                        wqk_part(r // NCH + 1, part_count)

            for s in range(PRO_A):
                step_a(s, s % 8, None)
            with pool.Fori(0, LOOP_A) as i:
                for r in range(8):
                    step_a(8 * i + (PRO_A + r), (PRO_A + r) % 8, 2 * i + (5 + r // NCH))

            def wvo_part(r, part, count):
                pool.wait_ge(wvo_hi, count)
                w = (wv, wo)[part][r % 2]
                pool.tensor_tensor(w[:, 1, :], w_raw[:, part, :], w[:, 0, :].bitcast(F32), ALU.subtract).then_inc(wvo_lo, 1)

            for s in range(STEPS_A - NCH, STEPS_A):
                step_a(s, s % 8, None)
                if s == STEPS_A - 2:
                    wvo_part(0, 0, 1)
            wvo_part(0, 1, 2)
            pool.wait_ge(stat_done, 1)
            pool.memset(pt[:, :, :, :, :], 0.0).then_inc(pt_zero, 1)

            def scale_scores(q, qr, load_count):
                pool.wait_ge(sc_loaded[qr % 2], load_count)
                v = sc[:, qr % 2, :].rearrange("p (h n) -> p h n", h=2)
                pool.tensor_tensor(v, v, rqk[:, :].unsqueeze(1).broadcast_to([P, 2, NT * C]), ALU.mult)\
                    .then_inc(sm_scaled, 1)

            def normalise(q, qr):
                pool.wait_ge(sm_rinv, q)
                v = sc[:, qr % 2, :].rearrange("p (m k) -> p m k", k=C)
                pool.tensor_tensor(v, v, rinv[:, :].unsqueeze(2).broadcast_to([P, 2 * NT, C]), ALU.mult)\
                    .then_inc(p_ready, 1)

            def pair_b(q, qr, load_count, part_count):
                scale_scores(q, qr, load_count)
                wvo_part(qr, 0, part_count)
                wvo_part(qr, 1, part_count + 1)
                normalise(q, qr)

            pool.wait_ge(rqk_ready, len(FIRST))
            for q in (1, 2):
                pair_b(q, q, 16 * (q // 2 + 1), 2 * q + 1)
            with pool.Fori(0, LOOP_B) as i:
                for r in range(2):
                    pair_b(2 * i + (3 + r), 3 + r, 16 * i + (32 + 16 * r), 4 * i + (7 + 2 * r))
            pair_b(NP - 1, NP - 1, 16 * (NP // 2), 2 * NP - 1)

        @block.vector
        def _(dve):
            chained = [0]

            def link(ins):
                chained[0] += 1
                ins.then_inc(chain, 1)
                dve.wait_ge(chain, chained[0])

            dve.wait_ge(ld_cond, 32)
            dve.wait_ge(iota_done, 1)
            link(dve.tensor_copy(idx_f[:, :], idx_i[:, :]))
            link(dve.tensor_copy(row_f[:, :], row_i[:, :]))
            dve.tensor_scalar(onehot[:, :], idx_f[:, :], row_f[:, 0:1], None, ALU.is_equal).then_inc(onehot_done, 1)

            def keep_scores(s, r, spill_count):
                hs, n = (r // NCH) % 2, r % NCH
                dve.wait_ge(scores_done, s + 1)
                if n == 0 and spill_count is not None:
                    dve.wait_ge(spilled[hs], spill_count)
                for j in range(NB):
                    rows = slice(j * C, (j + 1) * C)
                    src = bank[4 + r % 2][rows, :].rearrange("p (t n) -> p t n", t=TC)[:, :, j * C:(j + 1) * C]
                    dst = stage[rows, hs, n * TC * C:(n + 1) * TC * C].rearrange("p (t k) -> p t k", t=TC)
                    ins = dve.tensor_copy(dst, src)
                ins.then_inc(scores_kept, 1)

            dve.wait_ge(mix_raw, 1)
            dve.wait_ge(mix_zero, 1)
            for q in (0, 1):
                for j in range(NB):
                    dst, src = mix_block(q, j)
                    dve.tensor_copy(dst, src).then_inc(mix_done, 1)

            def mix_lo(n):
                c, i = n // KI, n % KI
                dve.wait_ge(xc_hi_done, n + 1)
                cols = slice(c * CH, (c + 1) * CH)
                dve.tensor_tensor(xc_lo[:, i, cols], bank[mix_bank(n)][:, :], xc_hi[:, i, cols].bitcast(F32),
                                  ALU.subtract).then_inc(xc_lo_done, 1)

            for n in range(2 * KI):
                mix_lo(n)
                if n == 0:
                    dve.wait_ge(ld_vec, 16)
                    dve.tensor_tensor(vec[:, :, 3], vec[:, :, 3], vec[:, :, 4], ALU.mult).then_inc(vec_ready, 1)
                    dve.wait_ge(vec_ready, 1)
                    dve.tensor_tensor(vec[:, :, 4], vec[:, :, 0], vec[:, :, 3], ALU.mult).then_inc(vec_ready, 1)
            for n in range(2 * KI, 3 * KI):
                mix_lo(n)
            keep_scores(0, 0, None)
            for n in range(3 * KI, 4 * KI):
                mix_lo(n)
            keep_scores(1, 1, None)

            dve.wait_ge(ld_code, 32)
            link(dve.tensor_reduce(cbmax[:, 0:1], cb[:, :], AX, ALU.max, apply_absolute_value=True))
            link(dve.tensor_scalar(cbmax[:, 0:1], cbmax[:, 0:1], 1e-8, None, ALU.max))
            link(dve.reciprocal(cbmax[:, 1:2], cbmax[:, 0:1]))
            link(dve.tensor_scalar(cb[:, :], cb[:, :], cbmax[:, 1:2], None, ALU.mult))
            link(dve.tensor_tensor(step[:, 0:NCODE - 1], cb[:, 1:NCODE], cb[:, 0:NCODE - 1], ALU.subtract))
            link(dve.tensor_tensor(thr_t[:, 0:NCODE - 1], cb[:, 1:NCODE], cb[:, 0:NCODE - 1], ALU.add))
            link(dve.memset(thr[:, 0:1], -BIG))
            link(dve.memset(thr[:, NCODE:NCODE + 1], BIG))
            link(dve.tensor_scalar(thr[:, 1:NCODE], thr_t[:, 0:NCODE - 1], 0.5, None, ALU.mult))
            s = NCODE // 2
            while s >= 1:
                mid, low, high = thr[:, s:NCODE:2 * s], thr[:, 0:NCODE:2 * s], thr[:, 2 * s:NCODE + 1:2 * s]
                link(dve.tensor_tensor(mid, mid, low, ALU.max))
                link(dve.tensor_tensor(mid, mid, high, ALU.min))
                s //= 2
            link(dve.tensor_scalar(sl[:, :], sl[:, :], 88.0, -87.0, ALU.min, ALU.max))
            link(dve.tensor_scalar(ek[:, :], sl[:, :], LOG2E, MAGIC, ALU.mult, ALU.add))
            link(dve.tensor_scalar(ek[:, :], ek[:, :], MAGIC, None, ALU.subtract))
            link(dve.scalar_tensor_tensor(out=er[:, :], in0=ek[:, :], scalar=-LN2_HI, in1=sl[:, :], op0=ALU.mult, op1=ALU.add))
            link(dve.scalar_tensor_tensor(out=er[:, :], in0=ek[:, :], scalar=-LN2_LO, in1=er[:, :], op0=ALU.mult, op1=ALU.add))
            link(dve.tensor_scalar(ep[:, :], er[:, :], TAYLOR[0], None, ALU.mult))
            for coef in TAYLOR[1:]:
                link(dve.scalar_tensor_tensor(out=ep[:, :], in0=ep[:, :], scalar=coef, in1=er[:, :], op0=ALU.add, op1=ALU.mult))
            link(dve.tensor_scalar(ep[:, :], ep[:, :], 1.0, None, ALU.add))
            link(dve.tensor_scalar(ek[:, :], ek[:, :], 127.0, 8388608.0, ALU.add, ALU.mult))
            link(dve.tensor_copy(e2i[:, :], ek[:, :]))
            link(dve.tensor_tensor(gscale[:, :], ep[:, :], e2i[:, :].bitcast(F32), ALU.mult))
            link(dve.reciprocal(grec[:, :], gscale[:, :]))
            keep_scores(2, 2, None)
            keep_scores(3, 3, None)

            def normalised(ob):
                rows = qv[:, ob * D:(ob + 1) * D]
                kept = update[:, ob * D:(ob + 1) * D]
                dve.wait_ge(lora_done, ob + 1)
                dve.tensor_scalar(kept, bank[6 + ob % 2][:, :], LORA_SCALE, None, ALU.mult).then_inc(lora_used, 1)
                dve.wait_ge(lora_used, ob + 1)
                link(dve.tensor_tensor(rows, rows, kept, ALU.add))
                v = rows.rearrange("p (g n) -> p g n", g=G)
                link(dve.tensor_tensor(v, v, grec[:, ob * G:(ob + 1) * G].unsqueeze(2).broadcast_to([P, G, P]), ALU.mult))

            dve.wait_ge(ld_quant, 16 * 7)
            normalised(0)
            normalised(1)
            keep_scores(4, 4, None)
            keep_scores(5, 5, None)
            normalised(2)
            normalised(3)
            link(dve.tensor_scalar(qf[:, :], qv[:, :], 0.0, cb[:, 0:1], ALU.mult, ALU.add))

            def quantise(u, half, t):
                cols = slice(half * 1024, (half + 1) * 1024)
                if not isinstance(u, int) or u >= 1:
                    dve.wait_ge(quant_sum, u)
                dve.tensor_scalar(qm[:, :], qv[:, cols], thr[:, bass.ds(t + 1, 1)], step[:, bass.ds(t, 1)],
                                  ALU.is_gt, ALU.mult).then_inc(quant_mask, 1)
                dve.wait_ge(quant_mask, u + 1)
                dve.tensor_tensor(qf[:, cols], qf[:, cols], qm[:, :], ALU.add).then_inc(quant_sum, 1)

            units = 0
            for s in range(6, PRO_A):
                hh = s // NCH
                keep_scores(s, s % 8, 16 * (hh // 2) if hh >= 2 else None)
                for _ in range(3 if s < 6 + UNITS_PRO - 2 * (PRO_A - 6) else 2):
                    quantise(units, units % 2, units // 2)
                    units += 1
            dve.wait_ge(ld_res, 16)
            for i in range(KI):
                dve.tensor_scalar(xr[:, i, :], xr[:, i, :], bo_sb[:, i:i + 1], None, ALU.add).then_inc(res_ready, 1)
            with dve.Fori(0, LOOP_A) as i:
                for r in range(8):
                    keep_scores(8 * i + (PRO_A + r), (PRO_A + r) % 8, 16 * i + (16 + 16 * (r // NCH)))
                    quantise(8 * i + (UNITS_PRO + r), r % 2, dve.snap(4 * i + (UNITS_PRO // 2 + r // 2)))
            n_units = 2 * (NCODE - 1)
            for s in range(STEPS_A - NCH, STEPS_A):
                keep_scores(s, s % 8, 16 * (s // NCH // 2))
                if s == STEPS_A - 4:
                    dve.wait_ge(quant_sum, n_units)
                    link(dve.tensor_tensor(qf[:, :], qf[:, :], qv[:, :], ALU.subtract))
                    link(dve.tensor_tensor(qf[:, :], qf[:, :], qv[:, :], ALU.add))
                if s == STEPS_A - 3:
                    v = qf[:, :].rearrange("p (m n) -> p m n", n=P)
                    link(dve.tensor_tensor(v, v, gscale[:, :].unsqueeze(2).broadcast_to([P, KI * G, P]), ALU.mult))
                    dve.tensor_tensor(qf[:, :], qf[:, :], update, ALU.add).then_inc(w_eff_done, 1)

            dve.wait_ge(stat_done, 1)
            dve.tensor_scalar(qv1[:, :], bank[4][:, 0:NT], 1.0 / INNER, EPS, ALU.mult, ALU.add).then_inc(var_ready, 1)
            for t0, t1 in FIRST:
                dve.tensor_scalar(kv[:, t0 * C:t1 * C], bank[5][:, t0 * C:t1 * C], 1.0 / INNER, EPS, ALU.mult, ALU.add)\
                   .then_inc(var_ready, 1)

            def inverse_root(a, y, z):
                link(dve.reciprocal(y, y))
                link(dve.tensor_tensor(z, y, y, ALU.mult))
                link(dve.scalar_tensor_tensor(out=z, in0=z, scalar=-0.5, in1=a, op0=ALU.mult, op1=ALU.mult))
                link(dve.scalar_tensor_tensor(out=y, in0=z, scalar=1.5, in1=y, op0=ALU.add, op1=ALU.mult))

            def both_norms(part):
                t0, t1 = FIRST[part]
                keys = slice(t0 * C, t1 * C)
                dve.wait_ge(std_ready, 2 + part)
                inverse_root(kv[:, keys], kn[:, keys], kn2[:, keys])
                dve.tensor_tensor(rqk[:, keys].rearrange("p (t k) -> p t k", k=C),
                                  kn[:, keys].rearrange("p (t k) -> p t k", k=C),
                                  qn[:, t0:t1].unsqueeze(2).broadcast_to([P, t1 - t0, C]), ALU.mult).then_inc(rqk_ready, 1)
                dve.wait_ge(rqk_ready, part + 1)

            dve.wait_ge(std_ready, 1)
            inverse_root(qv1[:, :], qn[:, :], qn2[:, :])
            link(dve.tensor_scalar(qn[:, :], qn[:, :], SCORE_SCALE, None, ALU.mult))

            def shift(q, qr):
                v = sc[:, qr % 2, :].rearrange("p (m k) -> p m k", k=C)
                dve.wait_ge(sm_scaled, q)
                dve.tensor_reduce(mx[:, :], v, AX, ALU.max).then_inc(sm_max, 1)
                dve.wait_ge(sm_max, q)
                dve.tensor_tensor(v, v, mx[:, :].unsqueeze(2).broadcast_to([P, 2 * NT, C]), ALU.subtract)\
                   .then_inc(sm_shift, 1)

            def invert(q, qr):
                v = sc[:, qr % 2, :].rearrange("p (m k) -> p m k", k=C)
                dve.wait_ge(sm_exp, q)
                dve.tensor_reduce(rsum[:, :], v, AX, ALU.add).then_inc(sm_sum, 1)
                dve.wait_ge(sm_sum, q)
                dve.reciprocal(rinv[:, :], rsum[:, :]).then_inc(sm_rinv, 1)

            def transpose_p(g, r, pair_count=None):
                if r % NCH == 0 and pair_count is not None:
                    dve.wait_ge(p_ready, pair_count - 1)
                if not isinstance(g, int) or g >= 2:
                    dve.wait_ge(pv_done, 2 * g - 2)
                n = r % NCH
                for j in range(NB):
                    rows = slice(j * C, (j + 1) * C)
                    src = sc[rows, (r // NCH) % 2, :].rearrange("p (h t k) -> p h t k", h=2, t=NT)[:, :, n * TC:(n + 1) * TC, :]
                    dst = pt[rows, r % 2, :, :, j * C:(j + 1) * C]
                    ins = dve.transpose(dst, src)
                ins.then_inc(pt_ready, 1)

            def out_lo(g, r, h):
                dve.wait_ge(o_hi, 2 * g + (h + 1))
                if h == 0 and (not isinstance(g, int) or g >= 2):
                    dve.wait_ge(wo_done, 4 * g - 4)
                dve.scalar_tensor_tensor(out=ot_lo[:, r % 2, h, :], in0=bank[2 + h][:, :], scalar=bvp[:, (r // NCH) % 2, h:h + 1],
                                         in1=ot_hi[:, r % 2, h, :].bitcast(F32), op0=ALU.add, op1=ALU.subtract)\
                   .then_inc(o_lo, 1)

            def add_out(g, r):
                n = r % NCH
                for i in range(KI):
                    dve.wait_ge(wo_done, 4 * g + (i + 1))
                    if not isinstance(g, int) or g >= 4:
                        dve.wait_ge(wo_added, 4 * g + (i - 15))
                    a = xr[:, i, n * CH:(n + 1) * CH]
                    dve.tensor_tensor(a, bank[4 + i][:, :], a, ALU.add).then_inc(wo_added, 1)

            def first_part(part):
                t0, t1 = FIRST[part]
                v = sc[:, 0, :].rearrange("p (h t k) -> p h t k", h=2, t=NT)[:, :, t0:t1, :]
                of_row = lambda a: a[:, :].rearrange("p (h t) -> p h t", h=2)[:, :, t0:t1]
                return v, of_row, lambda a: of_row(a).unsqueeze(3).broadcast_to([P, 2, t1 - t0, C])

            def first_shift(part):
                v, of_row, over_keys = first_part(part)
                t0, t1 = FIRST[part]
                for h in range(2):
                    scores = sc[:, 0, (h * NT + t0) * C:(h * NT + t1) * C]
                    ins = dve.tensor_tensor(scores, scores, rqk[:, t0 * C:t1 * C], ALU.mult)
                link(ins)
                link(dve.tensor_reduce(of_row(mx), v, AX, ALU.max))
                dve.tensor_tensor(v, v, over_keys(mx), ALU.subtract).then_inc(first_shifted, 1)

            def first_normalise(part):
                v, of_row, over_keys = first_part(part)
                dve.wait_ge(first_exp, part + 1)
                link(dve.tensor_reduce(of_row(rsum), v, AX, ALU.add))
                link(dve.reciprocal(of_row(rinv), of_row(rsum)))
                link(dve.tensor_tensor(v, v, over_keys(rinv), ALU.mult))

            both_norms(0)
            dve.wait_ge(sc_loaded[0], 16)
            first_shift(0)
            both_norms(1)
            first_normalise(0)
            dve.wait_ge(pt_zero, 1)
            dve.wait_ge(res_ready, KI)
            transpose_p(0, 0)
            first_shift(1)
            first_normalise(1)
            transpose_p(1, 1)
            out_lo(0, 0, 0)
            out_lo(0, 0, 1)
            both_norms(2)
            first_shift(2)
            first_normalise(2)

            def step_b(g, r, pair, last=False):
                static = isinstance(g, int)
                if not static or g >= 1:
                    out_lo(g - 1, r + 7, 0)
                    out_lo(g - 1, r + 7, 1)
                transpose_p(g, r, pair)
                if not last:
                    if r % NCH == 1:
                        shift(pair, r // NCH + 1)
                    if r % NCH == 2 and not (static and g == 2):
                        invert(pair, r // NCH + 1)
                if not static or g >= 2:
                    add_out(g - 2, r + 6)
                if static and g == 2:
                    shift(pair, 1)
                    invert(pair, 1)

            for g in range(2, PRO_B):
                step_b(g, g, g // NCH + 1)
            with dve.Fori(0, LOOP_B) as i:
                for r in range(8):
                    step_b(8 * i + (PRO_B + r), r, 2 * i + (3 + r // NCH))
            for g in range(PRO_B + 8 * LOOP_B, STEPS_B):
                step_b(g, g % 8, g // NCH + 1, last=g // NCH == NP - 1)
            last = STEPS_B - 1

            def expert_scores(c):
                if c >= 1:
                    dve.wait_ge(low_scaled, c)
                dve.wait_ge(rl_done, c + 1)
                for b2 in range(2):
                    ins = dve.tensor_copy(rl[:, 2 * b2:2 * b2 + 2, :],
                                          bank[b2][:, 0:2 * LR].rearrange("p (t n) -> p t n", t=2))
                ins.then_inc(rl_kept, 1)
                dve.wait_ge(rl_kept, c + 1)
                logit = rl[:, :, E_ * R_:LR]
                link(dve.tensor_tensor(lex, logit, br_sb[:, :].unsqueeze(1).broadcast_to([P, TC, E_]), ALU.add))
                link(dve.tensor_reduce(lmx[:, 0:TC], lex, AX, ALU.max))
                dve.tensor_tensor(lex, lex, lmx[:, 0:TC].unsqueeze(2).broadcast_to([P, TC, E_]), ALU.subtract)\
                   .then_inc(logit_shift, 1)
                dve.wait_ge(logit_exp, c + 1)
                link(dve.tensor_reduce(lsum[:, 0:TC], lex, AX, ALU.add))
                link(dve.reciprocal(linv[:, 0:TC], lsum[:, 0:TC]))
                link(dve.scalar_tensor_tensor(out=lex, in0=lex, scalar=OUT_SCALE,
                                              in1=linv[:, 0:TC].unsqueeze(2).broadcast_to([P, TC, E_]),
                                              op0=ALU.mult, op1=ALU.mult))
                if c >= 1:
                    dve.wait_ge(lowt_raw, c)
                dve.tensor_tensor(low_s.rearrange("p t (e r) -> p t e r", e=E_),
                                  rl[:, :, 0:E_ * R_].rearrange("p t (e r) -> p t e r", e=E_),
                                  lex.unsqueeze(3).broadcast_to([P, TC, E_, R_]), ALU.mult).then_inc(low_scaled, 1)

            def add_experts(c, slices=range(KI)):
                for i in slices:
                    n = c * KI + i
                    dve.wait_ge(fin_raw, n + 1)
                    a = xr[:, i, c * CH:(c + 1) * CH]
                    dve.tensor_tensor(a, fin_bank(c, i)[:, :], a, ALU.add).then_inc(fin_done, 1)

            expert_scores(0)
            out_lo(last, last % 8, 0)
            out_lo(last, last % 8, 1)
            add_out(last - 1, (last - 1) % 8)
            expert_scores(1)
            add_experts(0, (0, 1))
            add_out(last, last % 8)
            add_experts(0, (2, 3))
            expert_scores(2)
            add_experts(1, (0, 1))
            expert_scores(3)
            add_experts(1, (2, 3))
            add_experts(2)
            add_experts(3)


def kernel(**inputs):
    import numpy as np
    import concourse.bacc as bacc
    from concourse.bass_utils import run_bass_kernel_spmd

    a = {k: np.asarray(v) for k, v in inputs.items()}
    x = a["x"].reshape(NT, P, D)
    cols = lambda v: v.reshape(-1, P).T
    slices = lambda w: w.reshape(KI, P, -1).transpose(1, 0, 2)
    wq, wk = (a[f"L0_attn_W{n}"].reshape(KI, P, H, DH).transpose(2, 1, 0, 3) for n in "qk")
    wv = a["L0_attn_Wv"].reshape(KI, P, NP, 2 * DH).transpose(2, 1, 0, 3).reshape(NP, P, -1)
    wo = a["L0_attn_Wo"].reshape(NP, 2, DH, D).transpose(0, 2, 1, 3).reshape(NP, P, -1)
    laid = {
        "x_nat": x.transpose(1, 0, 2),
        "x_tr": slices(x.reshape(TOK, D).T),
        "cond_w": a["L0_cond_weights"].transpose(0, 2, 1).reshape(S16, -1),
        "cond_idx": np.broadcast_to(a["itok_B_0_15"], (S16, B)),
        "codebook": np.broadcast_to(a["condB_codebook"], (P, NCODE)),
        "wqk": np.concatenate([wq, wk], axis=2).reshape(H, P, -1),
        "wvo": np.concatenate([wv, wo], axis=2),
        "vecs": np.stack([cols(a[f"L0_attn_{n}"]) for n in ("bq", "bk", "bv", "gq", "gk")], axis=2),
        "bo": cols(a["L0_attn_bo"]),
        "w2": slices(a["L0_cond2_weight"]).reshape(P, -1),
        "scale_log": slices(a["L0_cond2_scale_log"].reshape(D, G)).reshape(P, -1),
        "lora_a": a["L0_cond2_lora_A"],
        "lora_bt": a["L0_cond2_lora_B"].T,
        "awr": slices(np.concatenate([a["L0_ffn_A"].reshape(E_ * R_, D).T, a["L0_ffn_Wr"].T], axis=1)),
        "bmat": a["L0_ffn_B"].transpose(0, 2, 1).reshape(E_ * R_, D),
        "br": np.broadcast_to(a["L0_ffn_br"], (P, E_)),
    }
    nc = bacc.Bacc("TRN2", target_bir_lowering=False, num_devices=1)
    arrays, args = {}, []
    for name, v in laid.items():
        v = np.ascontiguousarray(v)
        arrays[f"in_{name}"] = v
        args.append(nc.dram_tensor(f"in_{name}", v.shape, mybir.dt.from_np(v.dtype), kind="ExternalInput").ap())
    out = nc.dram_tensor("out_t", (P, KI, TOK), F32, kind="ExternalOutput").ap()
    build(nc, *args, out)
    r = run_bass_kernel_spmd(nc, [arrays], core_ids=[0])
    got = r.results[0]["out_t"]
    return got.transpose(1, 0, 2).reshape(D, TOK).T.reshape(B, C, D)
```
